# Optimizing a Trainium2 kernel written in Bass

```python
import numpy as np
import jax
import jax.numpy as jnp

def _softmax(x, axis=-1):
    return jax.nn.softmax(x, axis=axis)

def _gelu(x):
    return jax.nn.gelu(x, approximate=True)

def _silu(x):
    return jax.nn.silu(x)

def _sigmoid(x):
    return jax.nn.sigmoid(x)

def _layernorm(x, axis=-1, eps=1e-05):
    m = jnp.mean(x, axis=axis, keepdims=True)
    v = jnp.var(x, axis=axis, keepdims=True)
    return (x - m) / jnp.sqrt(v + eps)

def _scatter_add(tgt, idx, src, axis=0):
    return tgt.at[idx].add(src)

def _segment_sum(src, seg, n):
    return jax.ops.segment_sum(src, seg, n)
kernel_name = 'mk_cond_resid_d4_seqx_r4_c8052f'

def setup_inputs(seed: int=0):
    np.random.seed(seed)
    _w = jnp.asarray

    def _rec_inputs():
        import jax
        import jax.numpy as jnp
        _rk = jax.random.key(seed)
        x = -0.0003929 + 0.9999 * jax.random.normal(jax.random.fold_in(_rk, 1), (2, 1024, 256), jnp.float32)
        _lenS = 1024 - jax.random.randint(jax.random.fold_in(_rk, 7), (2,), 0, max(1, 1024 // 4) + 1, jnp.int32)
        _lenS2 = 1024 - jax.random.randint(jax.random.fold_in(_rk, 8), (2,), 0, max(1, 1024 // 4) + 1, jnp.int32)
        itok_B_0_7 = jax.random.randint(jax.random.fold_in(_rk, 11), (2,), 0, 8, jnp.int32)
        itok_B_0_8 = jax.random.randint(jax.random.fold_in(_rk, 12), (2,), 0, 9, jnp.int32)
        itok_B_0_15 = jax.random.randint(jax.random.fold_in(_rk, 13), (2,), 0, 16, jnp.int32)
        return (x, itok_B_0_7, itok_B_0_8, itok_B_0_15)
    x, itok_B_0_7, itok_B_0_8, itok_B_0_15 = _rec_inputs()

    def _L0_cond_setup():
        import jax, jax.numpy as jnp
        import numpy as np
        S, O, H = (8, 256, 256)
        B, N = (32, 128)
        key = jax.random.key(seed)
        k1, k2, k3, k4 = jax.random.split(key, 4)
        x = jax.random.normal(k1, (B, N, H), dtype=jnp.float32)
        subject_id = jax.random.randint(k2, (B,), 0, S)
        wbound = jnp.sqrt(2.0 / 6.0) * jnp.sqrt(3.0 / H)
        weight = jax.random.uniform(k3, (S, O, H), minval=-wbound, maxval=wbound, dtype=jnp.float32)
        bbound = 1.0 / jnp.sqrt(H)
        bias = jax.random.uniform(k4, (S, O), minval=-bbound, maxval=bbound, dtype=jnp.float32)
        return {'x': x, 'subject_id': subject_id, 'weight': weight, 'bias': bias}
    _L0_cond_all = _L0_cond_setup()
    _L0_cond_in = {k: v for k, v in _L0_cond_all.items() if k in ('weight', 'bias')}
    del _L0_cond_all

    def _L1_cond_setup():
        import jax, jax.numpy as jnp
        import numpy as np
        LN_EPS = 1e-05
        key = jax.random.key(seed)
        ks = jax.random.split(key, 8)
        B, S, H, A, L = (32, 512, 256, 64, 10)
        return {'hidden_states': jax.random.normal(ks[0], (B, S, H), dtype=jnp.float32), 'language_ids': jax.random.randint(ks[1], (B,), 0, L, dtype=jnp.int64), 'W1': jax.random.normal(ks[2], (L, H, A), dtype=jnp.float32) * (1.0 / np.sqrt(H)), 'b1': jnp.zeros((L, A), dtype=jnp.float32), 'W2': jax.random.normal(ks[3], (L, A, H), dtype=jnp.float32) * (1.0 / np.sqrt(A)), 'b2': jnp.zeros((L, H), dtype=jnp.float32), 'gamma': jnp.ones((L, H), dtype=jnp.float32), 'beta': jnp.zeros((L, H), dtype=jnp.float32)}
    _L1_cond_all = _L1_cond_setup()
    _L1_cond_in = {k: v for k, v in _L1_cond_all.items() if k in ('W1', 'b1', 'W2', 'b2', 'gamma', 'beta')}
    del _L1_cond_all

    def _L2_cond_setup():
        import jax, jax.numpy as jnp
        import numpy as np
        B, N, DIM = (32, 256, 256)
        HID = 1024
        PART = 64
        OUT = 256
        SHARED = OUT - PART
        E = 16
        key = jax.random.key(seed)
        ks = jax.random.split(key, 8)
        s = 0.02
        return {'x': jax.random.normal(ks[0], (B, N, DIM), dtype=jnp.float32), 'indices': jax.random.randint(ks[1], (B,), 0, E, dtype=jnp.int64), 'fc1_w': jax.random.normal(ks[2], (HID, DIM), dtype=jnp.float32) * s, 'fc1_b': jnp.zeros((HID,), dtype=jnp.float32), 'fc2_w': jax.random.normal(ks[3], (SHARED, HID), dtype=jnp.float32) * s, 'fc2_b': jnp.zeros((SHARED,), dtype=jnp.float32), 'experts_w': jax.random.normal(ks[4], (E, PART, HID), dtype=jnp.float32) * s, 'experts_b': jnp.zeros((E, PART), dtype=jnp.float32)}
    _L2_cond_all = _L2_cond_setup()
    _L2_cond_in = {k: v for k, v in _L2_cond_all.items() if k in ('fc1_w', 'fc1_b', 'fc2_w', 'fc2_b', 'experts_w', 'experts_b')}
    del _L2_cond_all

    def _L3_cond_setup():
        import jax, jax.numpy as jnp
        import numpy as np
        B, S, D, F = (32, 128, 256, 1024)
        R_COMMON, R_DOMAIN, E = (16, 16, 8)
        ALPHA = 2.0

        def _expert_lora(x, expert_ids, Wa, Wb):
            Ab = Wa[expert_ids]
            Bb = Wb[expert_ids]
            low = jnp.einsum('bsd,brd->bsr', x, Ab)
            return ALPHA * jnp.einsum('bsr,bor->bso', low, Bb)
        key = jax.random.key(seed)
        ks = jax.random.split(key, 12)
        sd = lambda k, shape: jax.random.normal(k, shape, dtype=jnp.float32) * (1.0 / np.sqrt(shape[-1]))
        return {'hidden_states': jax.random.normal(ks[0], (B, S, D), dtype=jnp.float32), 'expert_ids': jax.random.randint(ks[1], (B,), 0, E, dtype=jnp.int32), 'wi': sd(ks[2], (F, D)), 'wo': sd(ks[3], (D, F)), 'common_wi_a': sd(ks[4], (R_COMMON, D)), 'common_wi_b': sd(ks[5], (F, R_COMMON)), 'common_wo_a': sd(ks[6], (R_COMMON, F)), 'common_wo_b': sd(ks[7], (D, R_COMMON)), 'experts_wi_a': sd(ks[8], (E, R_DOMAIN, D)), 'experts_wi_b': sd(ks[9], (F, R_DOMAIN)) * jnp.ones((E, 1, 1)) * 0.0 + sd(ks[9], (E, F, R_DOMAIN)), 'experts_wo_a': sd(ks[10], (E, R_DOMAIN, F)), 'experts_wo_b': sd(ks[11], (E, D, R_DOMAIN))}
    _L3_cond_all = _L3_cond_setup()
    _L3_cond_in = {k: v for k, v in _L3_cond_all.items() if k in ('wi', 'wo', 'common_wi_a', 'common_wi_b', 'common_wo_a', 'common_wo_b', 'experts_wi_a', 'experts_wi_b', 'experts_wo_a', 'experts_wo_b')}
    del _L3_cond_all
    return {'x': x, 'itok_B_0_7': itok_B_0_7, 'itok_B_0_8': itok_B_0_8, 'itok_B_0_15': itok_B_0_15, 'L0_cond_weight': _L0_cond_in['weight'], 'L0_cond_bias': _L0_cond_in['bias'], 'L1_cond_W1': _L1_cond_in['W1'], 'L1_cond_b1': _L1_cond_in['b1'], 'L1_cond_W2': _L1_cond_in['W2'], 'L1_cond_b2': _L1_cond_in['b2'], 'L1_cond_gamma': _L1_cond_in['gamma'], 'L1_cond_beta': _L1_cond_in['beta'], 'L2_cond_fc1_w': _L2_cond_in['fc1_w'], 'L2_cond_fc1_b': _L2_cond_in['fc1_b'], 'L2_cond_fc2_w': _L2_cond_in['fc2_w'], 'L2_cond_fc2_b': _L2_cond_in['fc2_b'], 'L2_cond_experts_w': _L2_cond_in['experts_w'], 'L2_cond_experts_b': _L2_cond_in['experts_b'], 'L3_cond_wi': _L3_cond_in['wi'], 'L3_cond_wo': _L3_cond_in['wo'], 'L3_cond_common_wi_a': _L3_cond_in['common_wi_a'], 'L3_cond_common_wi_b': _L3_cond_in['common_wi_b'], 'L3_cond_common_wo_a': _L3_cond_in['common_wo_a'], 'L3_cond_common_wo_b': _L3_cond_in['common_wo_b'], 'L3_cond_experts_wi_a': _L3_cond_in['experts_wi_a'], 'L3_cond_experts_wi_b': _L3_cond_in['experts_wi_b'], 'L3_cond_experts_wo_a': _L3_cond_in['experts_wo_a'], 'L3_cond_experts_wo_b': _L3_cond_in['experts_wo_b']}

def reference(x, itok_B_0_7, itok_B_0_8, itok_B_0_15, L0_cond_weight, L0_cond_bias, L1_cond_W1, L1_cond_b1, L1_cond_W2, L1_cond_b2, L1_cond_gamma, L1_cond_beta, L2_cond_fc1_w, L2_cond_fc1_b, L2_cond_fc2_w, L2_cond_fc2_b, L2_cond_experts_w, L2_cond_experts_b, L3_cond_wi, L3_cond_wo, L3_cond_common_wi_a, L3_cond_common_wi_b, L3_cond_common_wo_a, L3_cond_common_wo_b, L3_cond_experts_wi_a, L3_cond_experts_wi_b, L3_cond_experts_wo_a, L3_cond_experts_wo_b):
    import jax
    import jax.numpy as jnp

    def _L0_cond_ref(x, subject_id, weight, bias):
        import jax, jax.numpy as jnp
        import numpy as np
        S, O, H = (8, 256, 256)
        B, N = (32, 128)
        W = weight[subject_id]
        b = bias[subject_id]
        y = jnp.einsum('bnh,boh->bno', x, W) + b[:, None, :]
        return y

    def _L1_cond_ref(hidden_states, language_ids, W1, b1, W2, b2, gamma, beta):
        import jax, jax.numpy as jnp
        import numpy as np
        LN_EPS = 1e-05
        w1 = W1[language_ids]
        w2 = W2[language_ids]
        h = jnp.einsum('bsh,bha->bsa', hidden_states, w1) + b1[language_ids][:, None, :]
        h = jax.nn.relu(h)
        adapted = jnp.einsum('bsa,bah->bsh', h, w2) + b2[language_ids][:, None, :]
        x = hidden_states + adapted
        mean = jnp.mean(x, axis=-1, keepdims=True)
        var = jnp.mean(jnp.square(x - mean), axis=-1, keepdims=True)
        normed = (x - mean) * jax.lax.rsqrt(var + LN_EPS)
        return normed * gamma[language_ids][:, None, :] + beta[language_ids][:, None, :]

    def _L2_cond_ref(x, indices, fc1_w, fc1_b, fc2_w, fc2_b, experts_w, experts_b):
        import jax, jax.numpy as jnp
        import numpy as np
        B, N, DIM = (32, 256, 256)
        HID = 1024
        PART = 64
        OUT = 256
        SHARED = OUT - PART
        E = 16
        h = jax.nn.gelu(jnp.einsum('bnd,hd->bnh', x, fc1_w) + fc1_b, approximate=False)
        shared = jnp.einsum('bnh,sh->bns', h, fc2_w) + fc2_b
        We = experts_w[indices]
        be = experts_b[indices]
        expert_x = jnp.einsum('bnh,bph->bnp', h, We) + be[:, None, :]
        return jnp.concatenate([shared, expert_x], axis=-1)

    def _L3_cond_ref(hidden_states, expert_ids, wi, wo, common_wi_a, common_wi_b, common_wo_a, common_wo_b, experts_wi_a, experts_wi_b, experts_wo_a, experts_wo_b):
        import jax, jax.numpy as jnp
        import numpy as np
        B, S, D, F = (32, 128, 256, 1024)
        R_COMMON, R_DOMAIN, E = (16, 16, 8)
        ALPHA = 2.0

        def _expert_lora(x, expert_ids, Wa, Wb):
            Ab = Wa[expert_ids]
            Bb = Wb[expert_ids]
            low = jnp.einsum('bsd,brd->bsr', x, Ab)
            return ALPHA * jnp.einsum('bsr,bor->bso', low, Bb)
        x = hidden_states
        hidden_i = jnp.einsum('bsd,fd->bsf', x, wi)
        hidden_i += ALPHA * jnp.einsum('bsr,fr->bsf', jnp.einsum('bsd,rd->bsr', x, common_wi_a), common_wi_b)
        hidden_i += _expert_lora(x, expert_ids, experts_wi_a, experts_wi_b)
        hidden_i = jax.nn.relu(hidden_i)
        hidden_o = jnp.einsum('bsf,df->bsd', hidden_i, wo)
        hidden_o += ALPHA * jnp.einsum('bsr,dr->bsd', jnp.einsum('bsf,rf->bsr', hidden_i, common_wo_a), common_wo_b)
        hidden_o += _expert_lora(hidden_i, expert_ids, experts_wo_a, experts_wo_b)
        return hidden_o
    x = x + _L0_cond_ref(x, itok_B_0_7, L0_cond_weight, L0_cond_bias)
    x = x + _L1_cond_ref(x, itok_B_0_8, L1_cond_W1, L1_cond_b1, L1_cond_W2, L1_cond_b2, L1_cond_gamma, L1_cond_beta)
    x = x + _L2_cond_ref(x, itok_B_0_15, L2_cond_fc1_w, L2_cond_fc1_b, L2_cond_fc2_w, L2_cond_fc2_b, L2_cond_experts_w, L2_cond_experts_b)
    x = x + _L3_cond_ref(x, itok_B_0_7, L3_cond_wi, L3_cond_wo, L3_cond_common_wi_a, L3_cond_common_wi_b, L3_cond_common_wo_a, L3_cond_common_wo_b, L3_cond_experts_wi_a, L3_cond_experts_wi_b, L3_cond_experts_wo_a, L3_cond_experts_wo_b)
    return x

_drawn_inputs = setup_inputs


def setup_inputs(seed=0):
    import zlib

    import numpy as np

    out = dict(_drawn_inputs(seed))
    spreads = {'L1_cond_b1': (0.0, 0.38),
     'L1_cond_b2': (0.0, 0.1),
     'L1_cond_gamma': (1.0, 0.2),
     'L1_cond_beta': (0.0, 0.1),
     'L2_cond_fc1_b': (0.0, 0.412),
     'L2_cond_fc2_b': (0.0, 0.1),
     'L2_cond_experts_b': (0.0, 0.343)}
    factors = {}
    for name, (base, spread) in spreads.items():
        noise = np.random.default_rng([zlib.crc32(name.encode()), seed]).standard_normal(out[name].shape)
        drawn = base * np.exp(spread * noise) if base else spread * noise
        out[name] = jnp.asarray(drawn.astype(out[name].dtype))
    for name, factor in factors.items():
        out[name] = (out[name] * factor).astype(out[name].dtype)
    return out
```

```python
from contextlib import ExitStack

import concourse.bass as bass
from concourse import mybir

ALU = mybir.AluOpType
ACT = mybir.ActivationFunctionType
F32 = mybir.dt.float32
F32R = mybir.dt.float32r
I32 = mybir.dt.int32

P = 128
ALPHA = 2.0
LN_EPS = 1e-5
RAW_SLOTS = 4
RES_SLOTS = 3
HID_SLOTS = 3
RANK2 = 32

PHASES = [(2, 0), (2, 1), (3, 0), (2, 2), (3, 1), (2, 3), (3, 2), (3, 3)]
CHUNKS = 8
LAG = 2


def make_plan():
    plan = [("bias", 0), ("x_in", 0), ("w_plain", (0, "w0")), ("x_in_lo", 0),
            ("w_adapt", 0), ("w_plain", (0, "fc1_0")), ("l0", 0), ("w_plain", (0, "fc1_1")),
            ("x1_lo", 0), ("l1a", 0), ("w_plain", (0, "fc2_0")), ("h1_lo", 0),
            ("l1b", 0), ("w_plain", (0, "fc2_1")), ("ln_in", 0), ("lora_a", 0), ("ln_norm", 0),
            ("lora_b_wi", 0), ("ln_out", 0), ("lora_b_wo", 0), ("x2_lo", 0)]
    front = ["x_in", "x_in_lo", "l0", "x1_lo", "l1a", "h1_lo", "l1b", "ln_in", "ln_norm", "ln_out", "x2_lo"]
    extra = {}

    def put(at, name, arg):
        extra.setdefault(at, []).append((name, arg))

    def put_front(tile, slots):
        for name, at in zip(front, slots):
            put(at, name, tile)

    put_front(1, [0, 0, 1, 2, 3, 3, 4, 5, 5, 6, 7])
    for n, piece in enumerate(("wi_0", "wi_1", "wo_0", "wo_1")):
        put(8 + 2 * n, "w_turn", (0, piece))
        put(9 + 2 * n, "w_lora", (0, piece))
    put(9, "w_plain", (1, "w0"))
    put(9, "w_adapt", 1)
    put_front(2, [11, 12, 13, 14, 16, 16, 17, 18, 19, 20, 21])
    put(18, "w_plain", (1, "fc2_1"))
    put(20, "lora_a", 1)
    put(21, "lora_b_wi", 1)
    put(22, "lora_b_wo", 1)
    put_front(3, [24, 25, 26, 27, 29, 29, 30, 31, 32, 33, 34])
    for n, piece in enumerate(("wi_0", "wi_1", "wo_0", "wo_1")):
        put(40 + 2 * n, "w_turn", (1, piece))
        put(41 + 2 * n, "w_lora", (1, piece))
    for ph, (layer, tile) in enumerate(PHASES):
        if layer == 3:
            put(CHUNKS * ph + CHUNKS + LAG + 1, "out", tile)
    total = CHUNKS * len(PHASES)
    for g in range(total + LAG + 2):
        if g < total:
            plan.append(("up", g))
        plan += extra.get(g, [])
        if 1 <= g <= total:
            plan.append(("hid_lo", g - 1))
        if LAG <= g < total + LAG:
            plan.append(("down", g - LAG))
            if (g - LAG) % CHUNKS == CHUNKS - 1:
                plan.append(("res", (g - LAG) // CHUNKS))
        if g >= LAG + 1 and (g - LAG - 1) % CHUNKS == CHUNKS - 1:
            plan.append(("res_lo", (g - LAG - 1) // CHUNKS))
    return plan


PLAN = make_plan()
PAIR_STAGES = ("bias", "x_in", "w_plain", "l0", "l1a", "l1b", "ln_in", "ln_out", "lora_b_wi", "lora_b_wo",
               "w_turn", "w_lora", "out")
PAIR_NO = {stage: n for n, stage in enumerate(s for s in PLAN if s[0] in PAIR_STAGES)}
PIECES = [arg for name, arg in PLAN if name in ("w_plain", "w_turn")]
PIECE_NO = {arg: n for n, arg in enumerate(PIECES)}
PLAIN = [arg for name, arg in PLAN if name == "w_plain"]
TURNED = [arg for name, arg in PLAN if name == "w_turn"]


def build(nc, x, subj_idx, lang_idx, exp_idx, w0, b0, w1, b1, w2, b2, gamma, beta, fc1_w, fc1_b, fc2_w, fc2_b,
          ex_w, ex_b, wi, wo, cwi_a, cwi_b, cwo_a, cwo_b, ewi_a, ewi_b, ewo_a, ewo_b, out):
    B, S, D = x.shape
    F = fc1_w.shape[0]
    A = w1.shape[2]
    SHARED = fc2_w.shape[0]
    R = cwi_a.shape[0]
    K = D // P
    TOKENS = 512
    TILES = B * S // TOKENS
    BLK = TOKENS // P
    HALF = F // 2
    assert K == 2 and F == CHUNKS * P and 2 * A == P and D - SHARED == A and 2 * R == RANK2 and TILES == 4
    PER_BATCH = TILES // B
    x_rows = x.rearrange("b s d -> (b s) d")
    out_rows = out.rearrange("b s d -> (b s) d")
    n_pieces = len(PIECES)

    with ExitStack() as ctx:
        def sb(name, shape, dt=F32):
            return ctx.enter_context(nc.sbuf_tensor(name, shape, dt))

        def sem(name):
            return ctx.enter_context(nc.semaphore(name))

        w0_hi, w0_lo = (sb(f"w0_{n}", [P, K, D], F32R) for n in ("hi", "lo"))
        w1_hi, w1_lo = (sb(f"w1_{n}", [P, K, 2, A], F32R) for n in ("hi", "lo"))
        w2_both = sb("w2_both", [P, D], F32R)
        fc1_hi, fc1_lo = (sb(f"fc1_{n}", [P, K, F], F32R) for n in ("hi", "lo"))
        fc2_hi, fc2_lo = (sb(f"fc2_{n}", [P, CHUNKS, D], F32R) for n in ("hi", "lo"))
        wi_hi, wi_lo = (sb(f"wi_{n}", [P, K, F], F32R) for n in ("hi", "lo"))
        wo_hi, wo_lo = (sb(f"wo_{n}", [P, CHUNKS, D], F32R) for n in ("hi", "lo"))
        raw = sb("raw", [P, RAW_SLOTS, 1024])
        w1_raw = sb("w1_raw", [P, K, A])
        w2_raw = sb("w2_raw", [P, D])
        merged = sb("merged", [P, 2, 1024])
        la_raw = sb("la_raw", [3 * RANK2, D + F])
        la = sb("la", [3 * RANK2, D + F], F32R)
        lb_raw = sb("lb_raw", [P, 2, CHUNKS + K, R])
        lb_rep = sb("lb_rep", [P, CHUNKS + K, 3, 2, R])
        lb = sb("lb", [3 * RANK2, F + D], F32R)
        bias_raw = sb("bias_raw", [9 + 10 * B, P])
        bias = sb("bias", [P, 9 + 10 * B])
        idx = sb("idx", [1, 3 * B], I32)
        ident = sb("ident", [P, P])
        mhalf = sb("mhalf", [P, BLK])
        x_tok = sb("x_tok", [P, 2, BLK, D])
        xt = sb("xt", [P, K, TOKENS])
        x1 = sb("x1", [P, K, TOKENS])
        f_hi, f_lo = (sb(f"f_{n}", [P, K, TOKENS], F32R) for n in ("hi", "lo"))
        h1 = sb("h1", [P, TOKENS])
        h1_hi = sb("h1_hi", [P, TOKENS], F32R)
        h1_lo = sb("h1_lo", [A, TOKENS], F32R)
        stats = sb("stats", [P, BLK, 6])
        mv = sb("mv", [P, BLK, 2])
        var_eps = sb("var_eps", [P, BLK])
        rstd = sb("rstd", [P, BLK])
        res = sb("res", [P, RES_SLOTS, K, TOKENS])
        res_hi, res_lo = (sb(f"res_{n}", [P, RES_SLOTS, K, TOKENS], F32R) for n in ("hi", "lo"))
        hid = sb("hid", [P, 2, TOKENS])
        hid_hi, hid_lo = (sb(f"hid_{n}", [P, HID_SLOTS, TOKENS], F32R) for n in ("hi", "lo"))
        out_tok = sb("out_tok", [P, BLK, D])

        pairs = ctx.enter_context(nc.psum_tensor("pairs", [P, 2, 1024], F32))
        hid_ps = ctx.enter_context(nc.psum_tensor("hid_ps", [P, 2, TOKENS], F32))
        acc = ctx.enter_context(nc.psum_tensor("acc", [P, K, TOKENS], F32))

        idx_loaded = sem("idx_loaded")
        x_loaded = [sem(f"x_loaded{t}") for t in range(TILES)]
        raw_loaded = [sem(f"raw_loaded{r}") for r in range(RAW_SLOTS)]
        bias_loaded = sem("bias_loaded")
        adapt_loaded = [sem(f"adapt_loaded{b}") for b in range(B)]
        lora_loaded = [sem(f"lora_loaded{b}") for b in range(B)]
        out_stored = sem("out_stored")
        pair_full = sem("pair_full")
        up_done = sem("up_done")
        down_done = sem("down_done")
        acc_full = sem("acc_full")
        pair_free = [sem(f"pair_free{r}") for r in range(2)]
        hid_free = [sem(f"hid_free{r}") for r in range(2)]
        ident_zero = sem("ident_zero")
        consts_ready = sem("consts_ready")
        bias_ready = sem("bias_ready")
        plain_hi, plain_lo = sem("plain_hi"), sem("plain_lo")
        adapt_hi, adapt_lo = sem("adapt_hi"), sem("adapt_lo")
        turned = sem("turned")
        summed = sem("summed")
        merged_hi, merged_lo = sem("merged_hi"), sem("merged_lo")
        la_hi, la_lo = sem("la_hi"), sem("la_lo")
        lb_copied = sem("lb_copied")
        lb_hi, lb_lo = sem("lb_hi"), sem("lb_lo")
        x_hi, x_lo = sem("x_hi"), sem("x_lo")
        x1_full = sem("x1_full")
        x1_hi, x1_lo = sem("x1_hi"), sem("x1_lo")
        h1_full, h1_hi_s, h1_lo_s = sem("h1_full"), sem("h1_hi_s"), sem("h1_lo_s")
        s_full = sem("s_full")
        stat_step = sem("stat_step")
        rstd_ready = sem("rstd_ready")
        norm_ready = sem("norm_ready")
        affine_ready = sem("affine_ready")
        x2_full, x2_hi, x2_lo = sem("x2_full"), sem("x2_hi"), sem("x2_lo")
        hid_full = sem("hid_full")
        hid_hi_s, hid_lo_s = sem("hid_hi_s"), sem("hid_lo_s")
        res_full = sem("res_full")
        x3_hi, x3_lo = sem("x3_hi"), sem("x3_lo")
        out_copied = sem("out_copied")

        def bias_fc1(j):
            return bias[:, j:j + 1]

        def bias_of(b, what, c=0):
            first = 9 + 10 * b + {"b0": 0, "b1": 2, "b2": 3, "gamma": 5, "beta": 7, "fc2_1": 9}[what]
            return bias[:, first + c:first + c + 1]

        def bias_fc2(b, c):
            return bias[:, 8:9] if c == 0 else bias_of(b, "fc2_1")

        def pair(stage):
            return pairs[:, PAIR_NO[stage] % 2]

        def turned_no(arg):
            return TURNED.index(arg)

        phase_of = {lt: n for n, lt in enumerate(PHASES)}
        layer3_before = {ph: sum(1 for q in range(ph) if PHASES[q][0] == 3) for ph in range(len(PHASES) + 1)}
        layer2_before = {ph: ph - n for ph, n in layer3_before.items()}
        gelus = [g for g in range(CHUNKS * len(PHASES)) if PHASES[g // CHUNKS][0] == 2]

        def plain_dest(name):
            if name == "w0":
                return w0_hi[:], w0_lo[:]
            what, n = name.split("_")
            n = int(n)
            if what == "fc1":
                return fc1_hi[:, :, n * HALF:(n + 1) * HALF], fc1_lo[:, :, n * HALF:(n + 1) * HALF]
            return fc2_hi[:, :, n * P:(n + 1) * P], fc2_lo[:, :, n * P:(n + 1) * P]

        def merged_dest(name):
            what, n = name.split("_")
            n = int(n)
            if what == "wi":
                return wi_hi[:, :, n * HALF:(n + 1) * HALF], wi_lo[:, :, n * HALF:(n + 1) * HALF]
            h = CHUNKS // 2
            return wo_hi[:, n * h:(n + 1) * h, :], wo_lo[:, n * h:(n + 1) * h, :]

        def shaped(flat, name):
            if name == "w0":
                return flat[:, 0:K * D].rearrange("p (k n) -> p k n", k=K)
            what = name[:3]
            if what in ("fc1", "wi_"):
                return flat.rearrange("p (k n) -> p k n", k=K)
            if what == "fc2":
                return flat.rearrange("p (j n) -> p j n", j=CHUNKS)
            return flat.rearrange("p (j n) -> p j n", j=CHUNKS // 2)

        block = ctx.enter_context(nc.Block())

        @block.sync
        def _(sp):
            def load_x(t):
                if t >= 2:
                    sp.wait_ge(pair_full, PAIR_NO[("ln_out", t - 2)] + 1)
                sp.dma_start(x_tok[:, t % 2], x_rows[t * TOKENS:(t + 1) * TOKENS, :].rearrange(
                    "(p k) d -> p k d", k=BLK)).then_inc(x_loaded[t], 16)

            for n, source in enumerate((subj_idx, lang_idx, exp_idx)):
                sp.dma_start(idx[0:1, n * B:(n + 1) * B], source.rearrange("(a b) -> a b", a=1)).then_inc(idx_loaded, 16)
            load_x(0)
            sp.wait_ge(idx_loaded, 48)
            subj = [sp.value_load(idx[0:1, b:b + 1], min_val=0, max_val=w0.shape[0] - 1) for b in range(B)]
            lang = [sp.value_load(idx[0:1, B + b:B + b + 1], min_val=0, max_val=w1.shape[0] - 1) for b in range(B)]
            expert = [sp.value_load(idx[0:1, 2 * B + b:2 * B + b + 1], min_val=0, max_val=ex_w.shape[0] - 1)
                      for b in range(B)]

            def row(table, i):
                return table[bass.ds(i, 1)]

            def load_piece(n):
                b, name = PIECES[n]
                slot, done = raw[:, n % RAW_SLOTS], raw_loaded[n % RAW_SLOTS]
                if n >= RAW_SLOTS:
                    old = PIECES[n - RAW_SLOTS]
                    kind = "w_turn" if old in TURNED else "w_plain"
                    sp.wait_ge(pair_full, PAIR_NO[(kind, old)] + 1)
                what, _, half = name.partition("_")
                if name == "w0":
                    sp.dma_start(slot[:, 0:K * D].rearrange("p (c h) -> p c h", c=K),
                                 row(w0, subj[b]).rearrange("a (c p) h -> p (a c) h", p=P)).then_inc(done, 16)
                elif what in ("fc1", "wi"):
                    source = (fc1_w if what == "fc1" else wi)[int(half) * HALF:(int(half) + 1) * HALF, :]
                    sp.dma_start(slot.rearrange("p (c h) -> p c h", c=CHUNKS // 2),
                                 source.rearrange("(c p) h -> p c h", p=P)).then_inc(done, 16)
                elif name == "fc2_0":
                    sp.dma_start(slot, fc2_w[0:P, :]).then_inc(done, 16)
                elif name == "fc2_1":
                    sp.dma_start(slot[0:SHARED - P], fc2_w[P:SHARED, :]).then_inc(done, 16)
                    sp.dma_start(slot[SHARED - P:P], row(ex_w, expert[b]).rearrange("a p h -> (a p) h")).then_inc(done, 16)
                else:
                    sp.dma_start(slot.rearrange("p (c f) -> p c f", c=K),
                                 wo[:, int(half) * HALF:(int(half) + 1) * HALF].rearrange(
                                     "(c p) f -> p c f", p=P)).then_inc(done, 16)

            def load_bias():
                def to(first, rows, source):
                    sp.dma_start(bias_raw[first:first + rows, :], source.rearrange("(r p) -> r p", p=P)).then_inc(bias_loaded, 16)

                to(0, CHUNKS, fc1_b)
                to(CHUNKS, 1, fc2_b[0:P])
                for b in range(B):
                    at = 9 + 10 * b
                    for first, table, i in ((0, b0, subj), (3, b2, lang), (5, gamma, lang), (7, beta, lang)):
                        sp.dma_start(bias_raw[at + first:at + first + K, :],
                                     row(table, i[b]).rearrange("a (r p) -> (a r) p", p=P)).then_inc(bias_loaded, 16)
                    for half in range(2):
                        sp.dma_start(bias_raw[at + 2:at + 3, half * A:(half + 1) * A],
                                     row(b1, lang[b])).then_inc(bias_loaded, 16)
                    sp.dma_start(bias_raw[at + 9:at + 10, 0:SHARED - P],
                                 fc2_b[P:SHARED].rearrange("(r p) -> r p", r=1)).then_inc(bias_loaded, 16)
                    sp.dma_start(bias_raw[at + 9:at + 10, SHARED - P:P], row(ex_b, expert[b])).then_inc(bias_loaded, 16)

            def load_adapt(b):
                if b:
                    sp.wait_ge(adapt_hi, 3 * b)
                    sp.wait_ge(adapt_lo, 2 * b)
                sp.dma_start(w1_raw[:], row(w1, lang[b]).rearrange("a (k p) n -> p (a k) n", p=P)).then_inc(adapt_loaded[b], 16)
                for half in range(2):
                    sp.dma_start(w2_raw[half * A:(half + 1) * A, :],
                                 row(w2, lang[b]).rearrange("a p n -> (a p) n")).then_inc(adapt_loaded[b], 16)

            def load_lora(b):
                if b:
                    sp.wait_ge(la_hi, b)
                    sp.wait_ge(la_lo, b)
                    sp.wait_ge(lb_copied, 2 * b)
                for rep in range(3):
                    r = rep * RANK2
                    for n, source in enumerate((cwi_a, row(ewi_a, subj[b]).rearrange("a r d -> (a r) d"))):
                        sp.dma_start(la_raw[r + n * R:r + (n + 1) * R, 0:D], source).then_inc(lora_loaded[b], 16)
                    for n, source in enumerate((cwo_a, row(ewo_a, subj[b]).rearrange("a r d -> (a r) d"))):
                        sp.dma_start(la_raw[r + n * R:r + (n + 1) * R, D:D + F], source).then_inc(lora_loaded[b], 16)
                for n, source in enumerate((cwi_b, row(ewi_b, subj[b]).rearrange("a r d -> (a r) d"))):
                    sp.dma_start(lb_raw[:, n, 0:CHUNKS, :], source.rearrange("(p j) r -> p j r", j=CHUNKS)).then_inc(lora_loaded[b], 16)
                for n, source in enumerate((cwo_b, row(ewo_b, subj[b]).rearrange("a r d -> (a r) d"))):
                    sp.dma_start(lb_raw[:, n, CHUNKS:CHUNKS + K, :], source.rearrange("(p j) r -> p j r", j=K)).then_inc(lora_loaded[b], 16)

            load_piece(0)
            load_bias()
            load_piece(1)
            load_adapt(0)
            load_piece(2)
            load_piece(3)
            load_x(1)
            load_lora(0)
            piece = RAW_SLOTS
            for name, arg in PLAN:
                if name in ("w_plain", "w_turn") and piece < n_pieces and PIECE_NO[arg] + RAW_SLOTS == piece:
                    load_piece(piece)
                    piece += 1
                elif name == "ln_out" and arg + 2 < TILES:
                    load_x(arg + 2)
                elif name == "w_adapt" and arg + 1 < B:
                    load_adapt(arg + 1)
                elif name == "lora_b_wo" and arg + 1 < B:
                    load_lora(arg + 1)
                elif name == "out":
                    n = layer3_before[phase_of[(3, arg)]]
                    sp.wait_ge(out_copied, n + 1)
                    sp.dma_start(out_rows[arg * TOKENS:(arg + 1) * TOKENS, :].rearrange("(p k) d -> p k d", k=BLK),
                                 out_tok[:]).then_inc(out_stored, 16)
            sp.wait_ge(out_stored, 16 * TILES)

        @block.tensor
        def _(pe):
            mm = nc.tensor.matmul

            def exact(dst, w_hi, w_lo, a_hi, a_lo, start, stop):
                mm(dst, w_hi, a_hi, start=start, stop=False)
                mm(dst, w_hi, a_lo, start=False, stop=False)
                return mm(dst, w_lo, a_hi, start=False, stop=stop)

            def turn(dst, source):
                return nc.tensor.transpose(dst, source, ident[0:source.shape[0], 0:source.shape[0]])

            def wait_pair(stage):
                n = PAIR_NO[stage]
                if n >= 2:
                    pe.wait_ge(pair_free[n % 2], n // 2)

            for stage in PLAN:
                name, arg = stage
                if name in PAIR_STAGES:
                    wait_pair(stage)
                    dst = pair(stage)
                if name == "bias":
                    pe.wait_ge(consts_ready, 2)
                    pe.wait_ge(bias_loaded, 16 * (2 + 8 * B))
                    turn(dst[:, 0:9 + 10 * B], bias_raw[:]).then_inc(pair_full, 1)
                elif name == "x_in":
                    pe.wait_ge(x_loaded[arg], 16)
                    for k in range(K):
                        for i in range(BLK):
                            last = turn(dst[:, k * TOKENS + i * P:k * TOKENS + (i + 1) * P],
                                        x_tok[:, arg % 2, i, k * P:(k + 1) * P])
                    last.then_inc(pair_full, 1)
                elif name in ("w_plain", "w_turn"):
                    b, piece = arg
                    n = PIECE_NO[arg]
                    slot = raw[:, n % RAW_SLOTS]
                    loads = sum(2 if PIECES[q][1] == "fc2_1" else 1 for q in range(n % RAW_SLOTS, n + 1, RAW_SLOTS))
                    pe.wait_ge(raw_loaded[n % RAW_SLOTS], 16 * loads)
                    view = shaped(dst, piece)
                    if piece == "w0":
                        for k in range(K):
                            for c in range(K):
                                last = turn(view[:, k, c * P:(c + 1) * P], slot[:, c * D + k * P:c * D + (k + 1) * P])
                    elif piece[:2] in ("fc", "wi") and piece[:3] != "fc2":
                        for k in range(K):
                            for c in range(CHUNKS // 2):
                                last = turn(view[:, k, c * P:(c + 1) * P], slot[:, c * D + k * P:c * D + (k + 1) * P])
                    elif piece[:3] == "fc2":
                        for j in range(CHUNKS):
                            last = turn(view[:, j, :], slot[:, j * P:(j + 1) * P])
                    else:
                        for j in range(CHUNKS // 2):
                            for c in range(K):
                                last = turn(view[:, j, c * P:(c + 1) * P], slot[:, c * HALF + j * P:c * HALF + (j + 1) * P])
                    last.then_inc(pair_full, 1)
                elif name in ("lora_b_wi", "lora_b_wo"):
                    pe.wait_ge(lb_copied, 2 * (arg + 1))
                    first, n = (0, CHUNKS) if name == "lora_b_wi" else (CHUNKS, K)
                    for j in range(n):
                        last = turn(dst[0:3 * RANK2, j * P:(j + 1) * P],
                                    lb_rep[:, first + j].rearrange("p a b r -> p (a b r)"))
                    last.then_inc(pair_full, 1)
                elif name == "w_lora":
                    b, piece = arg
                    half = int(piece[3:])
                    pe.wait_ge(la_lo, b + 1)
                    pe.wait_ge(lb_lo, 2 * (b + 1))
                    if piece[:2] == "wi":
                        for k in range(K):
                            last = mm(dst[:, k * HALF:(k + 1) * HALF], la[:, k * P:(k + 1) * P],
                                      lb[:, half * HALF:(half + 1) * HALF], start=True, stop=True)
                    else:
                        for j in range(CHUNKS // 2):
                            f = D + half * HALF + j * P
                            last = mm(dst[:, j * D:(j + 1) * D], la[:, f:f + P], lb[:, F:F + D], start=True, stop=True)
                    last.then_inc(pair_full, 1)
                elif name == "l0":
                    pe.wait_ge(plain_lo, PLAIN.index((arg // PER_BATCH, "w0")) + 1)
                    pe.wait_ge(x_lo, arg + 1)
                    for c in range(K):
                        for k in range(K):
                            last = exact(dst[:, c * TOKENS:(c + 1) * TOKENS], w0_hi[:, k, c * P:(c + 1) * P],
                                         w0_lo[:, k, c * P:(c + 1) * P], f_hi[:, k], f_lo[:, k], k == 0, k == K - 1)
                    last.then_inc(pair_full, 1)
                elif name == "l1a":
                    pe.wait_ge(adapt_lo, 2 * (arg // PER_BATCH + 1))
                    pe.wait_ge(x1_lo, arg + 1)
                    for k in range(K):
                        last = exact(dst[:, 0:TOKENS], w1_hi[:, k].rearrange("p a n -> p (a n)"),
                                     w1_lo[:, k].rearrange("p a n -> p (a n)"), f_hi[:, k], f_lo[:, k], k == 0, k == K - 1)
                    last.then_inc(pair_full, 1)
                elif name == "l1b":
                    pe.wait_ge(h1_lo_s, arg + 1)
                    for c in range(K):
                        mm(dst[:, c * TOKENS:(c + 1) * TOKENS], w2_both[:, c * P:(c + 1) * P], h1_hi[:], start=True, stop=False)
                        last = mm(dst[:, c * TOKENS:(c + 1) * TOKENS], w2_both[0:A, c * P:(c + 1) * P], h1_lo[:], start=False, stop=True)
                    last.then_inc(pair_full, 1)
                elif name == "ln_in":
                    pe.wait_ge(s_full, K * (arg + 1))
                    for i in range(BLK):
                        for k in range(K):
                            last = turn(dst[:, i * D + k * P:i * D + (k + 1) * P], xt[:, k, i * P:(i + 1) * P])
                    last.then_inc(pair_full, 1)
                elif name == "ln_out":
                    pe.wait_ge(norm_ready, arg + 1)
                    for k in range(K):
                        for i in range(BLK):
                            last = turn(dst[:, k * TOKENS + i * P:k * TOKENS + (i + 1) * P], x_tok[:, arg % 2, i, k * P:(k + 1) * P])
                    last.then_inc(pair_full, 1)
                elif name == "out":
                    pe.wait_ge(res_full, K * (phase_of[(3, arg)] + 1))
                    for i in range(BLK):
                        for k in range(K):
                            last = turn(dst[:, i * D + k * P:i * D + (k + 1) * P],
                                        res[:, arg % RES_SLOTS, k, i * P:(i + 1) * P])
                    last.then_inc(pair_full, 1)
                elif name == "up":
                    ph, j = divmod(arg, CHUNKS)
                    layer, t = PHASES[ph]
                    b = t // PER_BATCH
                    if arg >= 2:
                        pe.wait_ge(hid_free[arg % 2], arg // 2)
                    if layer == 2:
                        if j == 0:
                            pe.wait_ge(x2_lo, t + 1)
                        if j % (CHUNKS // 2) == 0:
                            pe.wait_ge(plain_lo, PLAIN.index((0, f"fc1_{j // (CHUNKS // 2)}")) + 1)
                        w_hi, w_lo = fc1_hi, fc1_lo
                    else:
                        if j == 0:
                            pe.wait_ge(x3_lo, layer2_before[phase_of[(2, t)]] + 1)
                        if j % (CHUNKS // 2) == 0:
                            pe.wait_ge(merged_lo, turned_no((b, f"wi_{j // (CHUNKS // 2)}")) + 1)
                        w_hi, w_lo = wi_hi, wi_lo
                    s = t % RES_SLOTS
                    for k in range(K):
                        last = exact(hid_ps[:, arg % 2], w_hi[:, k, j * P:(j + 1) * P], w_lo[:, k, j * P:(j + 1) * P],
                                     res_hi[:, s, k], res_lo[:, s, k], k == 0, k == K - 1)
                    last.then_inc(up_done, 1)
                elif name == "down":
                    ph, j = divmod(arg, CHUNKS)
                    layer, t = PHASES[ph]
                    b = t // PER_BATCH
                    pe.wait_ge(hid_lo_s, arg + 1)
                    if layer == 2:
                        if j == 0:
                            pe.wait_ge(plain_lo, PLAIN.index((b, "fc2_1")) + 1)
                        w_hi, w_lo = fc2_hi, fc2_lo
                    else:
                        if j % (CHUNKS // 2) == 0:
                            pe.wait_ge(merged_lo, turned_no((b, f"wo_{j // (CHUNKS // 2)}")) + 1)
                        w_hi, w_lo = wo_hi, wo_lo
                    for c in range(K):
                        if j == 0 and ph:
                            pe.wait_ge(res_full, K * (ph - 1) + c + 1)
                        last = exact(acc[:, c], w_hi[:, j, c * P:(c + 1) * P], w_lo[:, j, c * P:(c + 1) * P],
                                     hid_hi[:, arg % HID_SLOTS], hid_lo[:, arg % HID_SLOTS], j == 0, j == CHUNKS - 1)
                        if j == CHUNKS - 1 and c < K - 1:
                            last.then_inc(acc_full, 1)
                    last.then_inc(down_done, 1)

        @block.scalar
        def _(act):
            fn = nc.scalar.activation

            def wait_full(stage):
                act.wait_ge(pair_full, PAIR_NO[stage] + 1)

            for stage in PLAN:
                name, arg = stage
                if name in PAIR_STAGES:
                    source, free = pair(stage), pair_free[PAIR_NO[stage] % 2]
                if name == "bias":
                    wait_full(stage)
                    fn(bias[:], source[:, 0:9 + 10 * B], ACT.Copy).then_inc(bias_ready, 1)
                    act.wait_ge(bias_ready, 1)
                    act.sem_inc(free, 1)
                elif name == "x_in":
                    wait_full(stage)
                    if arg:
                        act.wait_ge(x2_full, arg)
                        act.wait_ge(pair_full, PAIR_NO[("l1a", arg - 1)] + 1)
                    flat = xt[:].rearrange("p k n -> p (k n)")
                    fn(flat, source, ACT.Copy).then_inc(x_hi, 1)
                    fn(f_hi[:].rearrange("p k n -> p (k n)"), source, ACT.Copy).then_inc(x_hi, 1)
                    act.wait_ge(x_hi, 2 * (arg + 1))
                    act.sem_inc(free, 1)
                elif name == "w_plain":
                    b, piece = arg
                    wait_full(stage)
                    if piece == "w0" and b:
                        act.wait_ge(pair_full, PAIR_NO[("l0", b * PER_BATCH - 1)] + 1)
                    if piece == "fc2_1" and b:
                        act.wait_ge(down_done, CHUNKS * (phase_of[(2, b * PER_BATCH - 1)] + 1))
                    fn(plain_dest(piece)[0], shaped(source, piece), ACT.Copy).then_inc(plain_hi, 1)
                elif name == "w_adapt":
                    act.wait_ge(adapt_loaded[arg], 48)
                    if arg:
                        act.wait_ge(pair_full, PAIR_NO[("l1b", arg * PER_BATCH - 1)] + 1)
                    for half in range(2):
                        fn(w1_hi[:, :, half], w1_raw[:], ACT.Copy).then_inc(adapt_hi, 1)
                    fn(w2_both[:], w2_raw[:], ACT.Copy).then_inc(adapt_hi, 1)
                elif name == "l0":
                    act.wait_ge(x1_full, K * (arg + 1))
                    fn(f_hi[:], x1[:], ACT.Copy).then_inc(x1_hi, 1)
                elif name == "l1a":
                    wait_full(stage)
                    b = arg // PER_BATCH
                    if arg:
                        act.wait_ge(pair_full, PAIR_NO[("l1b", arg - 1)] + 1)
                    fn(h1[:], source[:, 0:TOKENS], ACT.Relu, bias=bias_of(b, "b1")).then_inc(h1_full, 1)
                    act.wait_ge(h1_full, arg + 1)
                    act.sem_inc(free, 1)
                    fn(h1_hi[:], h1[:], ACT.Copy).then_inc(h1_hi_s, 1)
                elif name == "ln_out":
                    wait_full(stage)
                    b = arg // PER_BATCH
                    for k in range(K):
                        fn(xt[:, k], source[:, k * TOKENS:(k + 1) * TOKENS], ACT.Identity, bias=bias_of(b, "beta", k),
                           scale=bias_of(b, "gamma", k)).then_inc(affine_ready, 1)
                    act.wait_ge(affine_ready, K * (arg + 1))
                    act.sem_inc(free, 1)
                    act.wait_ge(x2_full, arg + 1)
                    fn(res_hi[:, arg % RES_SLOTS], res[:, arg % RES_SLOTS], ACT.Copy).then_inc(x2_hi, 1)
                elif name == "lora_a":
                    act.wait_ge(lora_loaded[arg], 16 * 16)
                    if arg:
                        act.wait_ge(pair_full, PAIR_NO[("w_lora", (arg - 1, "wo_1"))] + 1)
                    fn(la[:], la_raw[:], ACT.Copy).then_inc(la_hi, 1)
                elif name in ("lora_b_wi", "lora_b_wo"):
                    wait_full(stage)
                    first, n, at = (0, CHUNKS, 0) if name == "lora_b_wi" else (CHUNKS, K, F)
                    fn(lb[:, at:at + n * P].rearrange("r (p j) -> r j p", j=n),
                       source[0:3 * RANK2, 0:n * P].rearrange("r (j p) -> r j p", j=n), ACT.Copy,
                       scale=ALPHA).then_inc(lb_hi, 1)
                elif name == "w_turn":
                    wait_full(stage)
                    n = turned_no(arg)
                    if n >= 2:
                        act.wait_ge(merged_lo, n - 1)
                    fn(merged[:, n % 2], source, ACT.Copy).then_inc(turned, 1)
                    act.wait_ge(turned, n + 1)
                    act.sem_inc(free, 1)
                elif name == "w_lora":
                    b, piece = arg
                    n = turned_no(arg)
                    act.wait_ge(summed, n + 1)
                    if b:
                        ph = phase_of[(3, b * PER_BATCH - 1)]
                        used = CHUNKS * ph + CHUNKS // 2 * (int(piece[3:]) + 1)
                        act.wait_ge(up_done if piece[:2] == "wi" else down_done, used)
                    fn(merged_dest(piece)[0], shaped(merged[:, n % 2], piece), ACT.Copy).then_inc(merged_hi, 1)
                elif name == "up":
                    ph, j = divmod(arg, CHUNKS)
                    layer, t = PHASES[ph]
                    act.wait_ge(up_done, arg + 1)
                    if arg >= HID_SLOTS:
                        act.wait_ge(down_done, arg - HID_SLOTS + 1)
                    dst = hid_hi[:, arg % HID_SLOTS]
                    if layer == 2:
                        n = gelus.index(arg)
                        if n >= 2:
                            act.wait_ge(hid_lo_s, gelus[n - 2] + 1)
                        fn(hid[:, n % 2], hid_ps[:, arg % 2], ACT.Gelu, bias=bias_fc1(j)).then_inc(hid_full, 1)
                        act.wait_ge(hid_full, n + 1)
                        act.sem_inc(hid_free[arg % 2], 1)
                        fn(dst, hid[:, n % 2], ACT.Copy).then_inc(hid_hi_s, 1)
                    else:
                        fn(dst, hid_ps[:, arg % 2], ACT.Relu).then_inc(hid_hi_s, 1)
                elif name == "res":
                    layer, t = PHASES[arg]
                    if layer == 2:
                        act.wait_ge(res_full, K * (arg + 1))
                        fn(res_hi[:, t % RES_SLOTS], res[:, t % RES_SLOTS], ACT.Copy).then_inc(x3_hi, 1)
                elif name == "out":
                    wait_full(stage)
                    n = layer3_before[phase_of[(3, arg)]]
                    if n:
                        act.wait_ge(out_stored, 16 * n)
                    fn(out_tok[:].rearrange("p k d -> p (k d)"), source, ACT.Copy).then_inc(out_copied, 1)
                    act.wait_ge(out_copied, n + 1)
                    act.sem_inc(free, 1)

        @block.vector
        def _(dve):
            v = nc.vector

            def wait_full(stage):
                dve.wait_ge(pair_full, PAIR_NO[stage] + 1)

            for stage in PLAN:
                name, arg = stage
                if name in PAIR_STAGES:
                    source, free = pair(stage), pair_free[PAIR_NO[stage] % 2]
                if name == "bias":
                    v.memset(mhalf[:], -0.5).then_inc(consts_ready, 1)
                elif name == "w_plain":
                    b, piece = arg
                    n = PLAIN.index(arg)
                    dve.wait_ge(plain_hi, n + 1)
                    hi, lo = plain_dest(piece)
                    v.tensor_tensor(lo, shaped(source, piece), hi.bitcast(F32), ALU.subtract).then_inc(plain_lo, 1)
                    dve.wait_ge(plain_lo, n + 1)
                    dve.sem_inc(free, 1)
                elif name == "w_adapt":
                    dve.wait_ge(adapt_hi, 3 * (arg + 1))
                    for half in range(2):
                        last = v.tensor_tensor(w1_lo[:, :, half], w1_raw[:], w1_hi[:, :, half].bitcast(F32), ALU.subtract)
                    last.then_inc(adapt_lo, 1)
                    v.tensor_tensor(w2_both[A:2 * A], w2_raw[A:2 * A], w2_both[A:2 * A].bitcast(F32),
                                    ALU.subtract).then_inc(adapt_lo, 1)
                elif name == "l0":
                    wait_full(stage)
                    b = arg // PER_BATCH
                    dve.wait_ge(bias_ready, 1)
                    for k in range(K):
                        v.scalar_tensor_tensor(out=x1[:, k], in0=source[:, k * TOKENS:(k + 1) * TOKENS],
                                               scalar=bias_of(b, "b0", k), in1=xt[:, k], op0=ALU.add,
                                               op1=ALU.add).then_inc(x1_full, 1)
                    dve.wait_ge(x1_full, K * (arg + 1))
                    dve.sem_inc(free, 1)
                elif name == "x_in_lo":
                    dve.wait_ge(x_hi, 2 * (arg + 1))
                    v.tensor_tensor(f_lo[:], xt[:], f_hi[:].bitcast(F32), ALU.subtract).then_inc(x_lo, 1)
                elif name == "x1_lo":
                    dve.wait_ge(x1_hi, arg + 1)
                    v.tensor_tensor(f_lo[:], x1[:], f_hi[:].bitcast(F32), ALU.subtract).then_inc(x1_lo, 1)
                elif name == "h1_lo":
                    dve.wait_ge(h1_hi_s, arg + 1)
                    v.tensor_tensor(h1_lo[:], h1[0:A], h1_hi[0:A].bitcast(F32), ALU.subtract).then_inc(h1_lo_s, 1)
                elif name == "l1b":
                    wait_full(stage)
                    b = arg // PER_BATCH
                    for k in range(K):
                        v.scalar_tensor_tensor(out=xt[:, k], in0=source[:, k * TOKENS:(k + 1) * TOKENS],
                                               scalar=bias_of(b, "b2", k), in1=x1[:, k], op0=ALU.add,
                                               op1=ALU.add).then_inc(s_full, 1)
                    dve.wait_ge(s_full, K * (arg + 1))
                    dve.sem_inc(free, 1)
                elif name == "ln_in":
                    wait_full(stage)
                    done = (2 * BLK + 1) * arg
                    for i in range(BLK):
                        v.bn_stats(stats[:, i, :], source[:, i * D:(i + 1) * D]).then_inc(stat_step, 1)
                    dve.wait_ge(stat_step, done + BLK)
                    for i in range(BLK):
                        v.bn_aggr(mv[:, i, :], stats[:, i, :]).then_inc(stat_step, 1)
                    dve.wait_ge(stat_step, done + 2 * BLK)
                    v.tensor_scalar(var_eps[:], mv[:, :, 1], LN_EPS, None, ALU.add).then_inc(stat_step, 1)
                elif name == "ln_norm":
                    dve.wait_ge(rstd_ready, arg + 1)
                    ps, done = pair(("ln_in", arg)), pair_free[PAIR_NO[("ln_in", arg)] % 2]
                    for i in range(BLK):
                        last = v.tensor_scalar(x_tok[:, arg % 2, i, :], ps[:, i * D:(i + 1) * D], mv[:, i, 0:1],
                                               rstd[:, i:i + 1], ALU.subtract, ALU.mult)
                    last.then_inc(norm_ready, 1)
                    dve.wait_ge(norm_ready, arg + 1)
                    dve.sem_inc(done, 1)
                elif name == "ln_out":
                    dve.wait_ge(affine_ready, K * (arg + 1))
                    if arg >= RES_SLOTS:
                        dve.wait_ge(pair_full, PAIR_NO[("out", arg - RES_SLOTS)] + 1)
                    v.tensor_tensor(res[:, arg % RES_SLOTS], xt[:], x1[:], ALU.add).then_inc(x2_full, 1)
                elif name == "x2_lo":
                    dve.wait_ge(x2_hi, arg + 1)
                    s = arg % RES_SLOTS
                    v.tensor_tensor(res_lo[:, s], res[:, s], res_hi[:, s].bitcast(F32), ALU.subtract).then_inc(x2_lo, 1)
                elif name == "lora_a":
                    dve.wait_ge(la_hi, arg + 1)
                    low = slice(2 * RANK2, 3 * RANK2)
                    v.tensor_tensor(la[low], la_raw[low], la[low].bitcast(F32), ALU.subtract).then_inc(la_lo, 1)
                    if arg:
                        dve.wait_ge(pair_full, PAIR_NO[("lora_b_wo", arg - 1)] + 1)
                    for n in range(2):
                        v.tensor_copy(lb_rep[:, :, :, n, :],
                                      lb_raw[:, n].unsqueeze(2).to_broadcast([P, CHUNKS + K, 3, R])).then_inc(lb_copied, 1)
                elif name in ("lora_b_wi", "lora_b_wo"):
                    done = 2 * arg + (name == "lora_b_wo")
                    dve.wait_ge(lb_hi, done + 1)
                    first, n, at = (0, CHUNKS, 0) if name == "lora_b_wi" else (CHUNKS, K, F)
                    view = lb[RANK2:2 * RANK2, at:at + n * P].rearrange("r (p j) -> r j p", j=n)
                    v.scalar_tensor_tensor(out=view, in0=source[RANK2:2 * RANK2, 0:n * P].rearrange("r (j p) -> r j p", j=n),
                                           scalar=ALPHA, in1=view.bitcast(F32), op0=ALU.mult,
                                           op1=ALU.subtract).then_inc(lb_lo, 1)
                    dve.wait_ge(lb_lo, done + 1)
                    dve.sem_inc(free, 1)
                elif name == "w_lora":
                    b, piece = arg
                    n = turned_no(arg)
                    wait_full(stage)
                    dve.wait_ge(turned, n + 1)
                    v.tensor_tensor(merged[:, n % 2], source, merged[:, n % 2], ALU.add).then_inc(summed, 1)
                    dve.wait_ge(summed, n + 1)
                    dve.sem_inc(free, 1)
                elif name == "hid_lo":
                    layer, t = PHASES[arg // CHUNKS]
                    dve.wait_ge(hid_hi_s, arg + 1)
                    s = arg % HID_SLOTS
                    if layer == 2:
                        v.tensor_tensor(hid_lo[:, s], hid[:, gelus.index(arg) % 2], hid_hi[:, s].bitcast(F32),
                                        ALU.subtract).then_inc(hid_lo_s, 1)
                    else:
                        v.scalar_tensor_tensor(out=hid_lo[:, s], in0=hid_ps[:, arg % 2], scalar=0.0,
                                               in1=hid_hi[:, s].bitcast(F32), op0=ALU.max,
                                               op1=ALU.subtract).then_inc(hid_lo_s, 1)
                        dve.wait_ge(hid_lo_s, arg + 1)
                        dve.sem_inc(hid_free[arg % 2], 1)
                elif name == "res":
                    layer, t = PHASES[arg]
                    s, b = t % RES_SLOTS, t // PER_BATCH
                    for c in range(K):
                        if c < K - 1:
                            dve.wait_ge(acc_full, arg + 1)
                        else:
                            dve.wait_ge(down_done, CHUNKS * (arg + 1))
                        if layer == 2:
                            v.scalar_tensor_tensor(out=res[:, s, c], in0=acc[:, c], scalar=bias_fc2(b, c),
                                                   in1=res[:, s, c], op0=ALU.add, op1=ALU.add).then_inc(res_full, 1)
                        else:
                            v.tensor_tensor(res[:, s, c], acc[:, c], res[:, s, c], ALU.add).then_inc(res_full, 1)
                elif name == "res_lo":
                    layer, t = PHASES[arg]
                    if layer == 2:
                        dve.wait_ge(x3_hi, layer2_before[arg] + 1)
                        s = t % RES_SLOTS
                        v.tensor_tensor(res_lo[:, s], res[:, s], res_hi[:, s].bitcast(F32), ALU.subtract).then_inc(x3_lo, 1)

        @block.gpsimd
        def _(pool):
            g = nc.gpsimd
            g.memset(ident[:], 0.0).then_inc(ident_zero, 1)
            pool.wait_ge(ident_zero, 1)
            g.affine_select(out=ident[:], in_=ident[:], compare_op=ALU.not_equal, fill=1.0, base=0,
                            pattern=[[-1, P]], channel_multiplier=1).then_inc(consts_ready, 1)
            pool.wait_ge(consts_ready, 2)
            for name, arg in PLAN:
                if name == "ln_in":
                    pool.wait_ge(stat_step, (2 * BLK + 1) * (arg + 1))
                    g.tensor_tensor(rstd[:], var_eps[:], mhalf[:], ALU.pow).then_inc(rstd_ready, 1)
                elif name == "w_lora":
                    n = turned_no(arg)
                    pool.wait_ge(merged_hi, n + 1)
                    hi, lo = merged_dest(arg[1])
                    g.tensor_tensor(lo, shaped(merged[:, n % 2], arg[1]), hi.bitcast(F32), ALU.subtract).then_inc(merged_lo, 1)


_INS = ['x', 'itok_B_0_7', 'itok_B_0_8', 'itok_B_0_15', 'L0_cond_weight', 'L0_cond_bias', 'L1_cond_W1', 'L1_cond_b1',
        'L1_cond_W2', 'L1_cond_b2', 'L1_cond_gamma', 'L1_cond_beta', 'L2_cond_fc1_w', 'L2_cond_fc1_b',
        'L2_cond_fc2_w', 'L2_cond_fc2_b', 'L2_cond_experts_w', 'L2_cond_experts_b', 'L3_cond_wi', 'L3_cond_wo',
        'L3_cond_common_wi_a', 'L3_cond_common_wi_b', 'L3_cond_common_wo_a', 'L3_cond_common_wo_b',
        'L3_cond_experts_wi_a', 'L3_cond_experts_wi_b', 'L3_cond_experts_wo_a', 'L3_cond_experts_wo_b']


def kernel(**inputs):
    import numpy as _np
    import concourse.bacc as _bacc
    from concourse import mybir as _mybir
    from concourse.bass_utils import run_bass_kernel_spmd as _run

    nc = _bacc.Bacc("TRN2", target_bir_lowering=False, num_devices=1)
    arrays, args = {}, []
    for name in _INS:
        a = _np.ascontiguousarray(inputs[name])
        arrays[f"in_{name}_dram"] = a
        args.append(nc.dram_tensor(f"in_{name}_dram", a.shape, _mybir.dt.from_np(a.dtype), kind="ExternalInput").ap())
    args.append(nc.dram_tensor("out_0_dram", inputs["x"].shape, _mybir.dt.float32, kind="ExternalOutput").ap())
    build(nc, *args)
    r = _run(nc, [arrays], core_ids=[0])
    return r.results[0]["out_0_dram"]
```

```python
from contextlib import ExitStack

import concourse.bass as bass
from concourse import mybir

ALU = mybir.AluOpType
ACT = mybir.ActivationFunctionType
F32 = mybir.dt.float32
F32R = mybir.dt.float32r
I32 = mybir.dt.int32

P = 128
ALPHA = 2.0
LN_EPS = 1e-5
RAW_SLOTS = 4
RES_SLOTS = 3
HID_SLOTS = 3
WARM_UP = 14
RANK2 = 32

PHASES = [(2, 0), (2, 1), (3, 0), (2, 2), (3, 1), (2, 3), (3, 2), (3, 3)]
CHUNKS = 8
LAG = 2


def make_plan():
    w0_, fc1_0, fc1_1, fc2_0, fc2_1 = ((0, piece) for piece in ("w0", "fc1_0", "fc1_1", "fc2_0", "fc2_1"))
    plan = [("x_in", 0), ("x_in_lo", 0), ("w_plain", w0_), ("x_in", 1), ("w_hi", w0_), ("w_lo", w0_), ("l0", 0),
            ("x_in_lo", 1), ("bias", 0), ("w_plain", fc1_0), ("x1", 0), ("w_adapt", 0), ("x1_hi", 0), ("x1_lo", 0),
            ("l1a", 0), ("w_hi", fc1_0), ("h1", 0), ("w_lo", fc1_0), ("w_plain", fc1_1), ("l0", 1), ("h1_lo", 0),
            ("l1b", 0), ("w_hi", fc1_1), ("w_lo", fc1_1), ("s", 0), ("w_plain", fc2_0), ("x1", 1), ("ln_in", 0),
            ("w_hi", fc2_0), ("x1_hi", 1), ("x1_lo", 1), ("w_plain", fc2_1), ("ln_norm", 0), ("l1a", 1), ("w_lo", fc2_0),
            ("w_hi", fc2_1), ("ln_out", 0), ("h1", 1), ("x2", 0), ("x2_hi", 0), ("x2_lo", 0), ("w_lo", fc2_1),
            ("h1_lo", 1)]
    extra = {}

    def put(at, name, arg):
        extra.setdefault(at, []).append((name, arg))

    def put_front(tile, first):
        for name, at in (("x_in", 0), ("x_in_lo", 1), ("l0", 2), ("x1", 2), ("x1_hi", 3), ("x1_lo", 4), ("l1a", 5),
                         ("h1", 5), ("h1_lo", 6), ("l1b", 6), ("s", 6), ("ln_in", 7), ("ln_norm", 8), ("ln_out", 9), ("x2", 10), ("x2_hi", 11),
                         ("x2_lo", 12)):
            put(first + at, name, tile)

    def put_merged(batch, first, step=2):
        for n, piece in enumerate(("wi_0", "wi_1", "wo_0", "wo_1")):
            put(first + step * n, "w_turn", (batch, piece))
            put(first + step * n + 1, "w_lora", (batch, piece))
            put(first + step * n + 2, "w_split", (batch, piece))

    for at, name in ((0, "l1b"), (0, "s"), (1, "ln_in"), (2, "ln_norm"), (3, "ln_out"), (3, "x2"), (4, "x2_hi"),
                     (5, "x2_lo")):
        put(at, name, 1)
    put(3, "lora_a", 0)
    put(4, "lora_b_wi", 0)
    put(5, "lora_b_wo", 0)
    put_merged(0, 6, 2)
    put(8, "bias", 1)
    for at, piece in ((9, "w0"), (18, "fc2_1")):
        put(at, "w_plain", (1, piece))
        put(at, "w_hi", (1, piece))
        put(at + 1, "w_lo", (1, piece))
    put(10, "w_adapt", 1)
    put_front(2, 11)
    put_front(3, 27)
    put(28, "lora_a", 1)
    put(30, "lora_b_wi", 1)
    put(32, "lora_b_wo", 1)
    put_merged(1, 40, 2)
    for ph, (layer, tile) in enumerate(PHASES):
        if layer == 3:
            put(CHUNKS * ph + CHUNKS + LAG, "out", tile)
    total = CHUNKS * len(PHASES)
    for g in range(total + LAG + 2):
        if g < total:
            plan.append(("up", g))
        if 1 <= g <= total:
            plan.append(("hid_lo", g - 1))
        if g >= LAG + 1 and (g - LAG - 1) % CHUNKS == CHUNKS - 1:
            plan.append(("res_lo", (g - LAG - 1) // CHUNKS))
        plan += extra.get(g, [])
        if LAG <= g < total + LAG:
            plan.append(("down", g - LAG))
            if (g - LAG) % CHUNKS == CHUNKS - 1:
                plan.append(("res", (g - LAG) // CHUNKS))
    return plan


PLAN = make_plan()
PAIR_STAGES = ("bias", "x_in", "w_plain", "l0", "l1a", "l1b", "ln_in", "ln_out", "lora_b_wi", "lora_b_wo",
               "w_turn", "w_lora", "out")
PAIR_NO = {stage: n for n, stage in enumerate(s for s in PLAN if s[0] in PAIR_STAGES)}
FIRST_UP = PLAN.index(("up", 0))


def make_areas():
    areas, last, count = {}, {}, [0, 0]
    for stage in PAIR_NO:
        early = stage[0] in ("w_plain", "bias") and PLAN.index(stage) < FIRST_UP
        area = 2 * early + count[early] % 2
        count[early] += 1
        areas[stage] = (area, last.get(area))
        last[area] = stage
    return areas


AREAS = make_areas()
GELUS = [g for g in range(CHUNKS * len(PHASES)) if PHASES[g // CHUNKS][0] == 2]
PIECES = [arg for name, arg in PLAN if name in ("w_plain", "w_turn")]
PIECE_NO = {arg: n for n, arg in enumerate(PIECES)}
PLAIN = [arg for name, arg in PLAN if name == "w_plain"]
TURNED = [arg for name, arg in PLAN if name == "w_turn"]


def build(nc, x, subj_idx, lang_idx, exp_idx, w0, b0, w1, b1, w2, b2, gamma, beta, fc1_w, fc1_b, fc2_w, fc2_b,
          ex_w, ex_b, wi, wo, cwi_a, cwi_b, cwo_a, cwo_b, ewi_a, ewi_b, ewo_a, ewo_b, out):
    B, S, D = x.shape
    F = fc1_w.shape[0]
    A = w1.shape[2]
    SHARED = fc2_w.shape[0]
    R = cwi_a.shape[0]
    K = D // P
    TOKENS = 512
    TILES = B * S // TOKENS
    BLK = TOKENS // P
    HALF = F // 2
    assert K == 2 and F == CHUNKS * P and 2 * A == P and D - SHARED == A and 2 * R == RANK2 and TILES == 4
    PER_BATCH = TILES // B
    x_rows = x.rearrange("b s d -> (b s) d")
    out_rows = out.rearrange("b s d -> (b s) d")
    n_pieces = len(PIECES)

    with ExitStack() as ctx:
        def sb(name, shape, dt=F32):
            return ctx.enter_context(nc.sbuf_tensor(name, shape, dt))

        def sem(name):
            return ctx.enter_context(nc.semaphore(name))

        w0_hi, w0_lo = (sb(f"w0_{n}", [P, K, D], F32R) for n in ("hi", "lo"))
        w1_hi, w1_lo = (sb(f"w1_{n}", [P, K, 2, A], F32R) for n in ("hi", "lo"))
        w2_both = sb("w2_both", [P, D], F32R)
        fc1_hi, fc1_lo = (sb(f"fc1_{n}", [P, K, F], F32R) for n in ("hi", "lo"))
        fc2_hi, fc2_lo = (sb(f"fc2_{n}", [P, CHUNKS, D], F32R) for n in ("hi", "lo"))
        wi_hi, wi_lo = (sb(f"wi_{n}", [P, K, F], F32R) for n in ("hi", "lo"))
        wo_hi, wo_lo = (sb(f"wo_{n}", [P, CHUNKS, D], F32R) for n in ("hi", "lo"))
        raw = sb("raw", [P, RAW_SLOTS, 1024])
        w1_raw = sb("w1_raw", [P, K, A])
        w2_raw = sb("w2_raw", [P, D])
        merged = sb("merged", [P, 2, 1024])
        la_raw = sb("la_raw", [3 * RANK2, D + F])
        la = sb("la", [3 * RANK2, D + F], F32R)
        lb_raw = sb("lb_raw", [P, 2, CHUNKS + K, R])
        lb_rep = sb("lb_rep", [P, CHUNKS + K, 3, 2, R])
        lb = sb("lb", [3 * RANK2, F + D], F32R)
        bias_raw = [sb(f"bias_raw{b}", [10 + 9 * (b == 0), P]) for b in range(B)]
        bias = sb("bias", [P, 9 + 10 * B])
        idx = sb("idx", [1, 3 * B], I32)
        ident = sb("ident", [P, P])
        mhalf = sb("mhalf", [P, BLK])
        table_warm = sb("table_warm", [P, 1])
        x_tok = sb("x_tok", [P, 2, BLK, D])
        xt = sb("xt", [P, 2, K, TOKENS])
        h1 = sb("h1", [A, TOKENS])
        h1_hi = sb("h1_hi", [P, TOKENS], F32R)
        h1_lo = sb("h1_lo", [A, TOKENS], F32R)
        stats = sb("stats", [P, BLK, 6])
        mv = sb("mv", [P, BLK, 2])
        var_eps = sb("var_eps", [P, BLK])
        rstd = sb("rstd", [P, BLK])
        res = sb("res", [P, RES_SLOTS, K, TOKENS])
        res_hi, res_lo = (sb(f"res_{n}", [P, RES_SLOTS, K, TOKENS], F32R) for n in ("hi", "lo"))
        hid = sb("hid", [P, 2, TOKENS])
        hid_hi, hid_lo = (sb(f"hid_{n}", [P, HID_SLOTS, TOKENS], F32R) for n in ("hi", "lo"))
        out_tok = sb("out_tok", [P, BLK, D])

        pairs = ctx.enter_context(nc.psum_tensor("pairs", [P, 2, 1024], F32))
        hid_ps = ctx.enter_context(nc.psum_tensor("hid_ps", [P, 2, TOKENS], F32))
        acc = ctx.enter_context(nc.psum_tensor("acc", [P, K, TOKENS], F32))

        subj_loaded = sem("subj_loaded")
        idx_loaded = sem("idx_loaded")
        x_loaded = [sem(f"x_loaded{t}") for t in range(TILES)]
        raw_loaded = [sem(f"raw_loaded{r}") for r in range(RAW_SLOTS)]
        bias_loaded = [sem(f"bias_loaded{b}") for b in range(B)]
        rest_loaded = [sem(f"rest_loaded{b}") for b in range(B)]
        adapt_loaded = [sem(f"adapt_loaded{b}") for b in range(B)]
        lora_loaded = [sem(f"lora_loaded{b}") for b in range(B)]
        out_stored = sem("out_stored")
        pair_full = sem("pair_full")
        up_done = sem("up_done")
        down_done = sem("down_done")
        acc_full = sem("acc_full")
        ident_zero = sem("ident_zero")
        ident_ready = sem("ident_ready")
        mhalf_ready = sem("mhalf_ready")
        bias_ready = sem("bias_ready")
        plain_hi, plain_lo = sem("plain_hi"), sem("plain_lo")
        adapt_hi, adapt_lo = sem("adapt_hi"), sem("adapt_lo")
        turned = sem("turned")
        summed = sem("summed")
        merged_hi, merged_lo = sem("merged_hi"), sem("merged_lo")
        la_hi, la_lo = sem("la_hi"), sem("la_lo")
        lb_copied = sem("lb_copied")
        lb_hi, lb_lo = sem("lb_hi"), sem("lb_lo")
        x_hi, x_lo = sem("x_hi"), sem("x_lo")
        x_full = sem("x_full")
        x1_full = sem("x1_full")
        x1_hi, x1_lo = sem("x1_hi"), sem("x1_lo")
        h1_full, h1_hi_s, h1_lo_s = sem("h1_full"), sem("h1_hi_s"), sem("h1_lo_s")
        s_full = sem("s_full")
        stat_step = sem("stat_step")
        rstd_ready = sem("rstd_ready")
        norm_ready = sem("norm_ready")
        affine_ready = sem("affine_ready")
        x2_full, x2_hi, x2_lo = sem("x2_full"), sem("x2_hi"), sem("x2_lo")
        hid_full = sem("hid_full")
        hid_hi_s, hid_lo_s = sem("hid_hi_s"), sem("hid_lo_s")
        res_full = sem("res_full")
        x3_hi, x3_lo = sem("x3_hi"), sem("x3_lo")
        out_copied = sem("out_copied")

        def bias_fc1(j):
            return bias[:, j:j + 1]

        def bias_of(b, what, c=0):
            first = 9 + 10 * b + {"b0": 0, "b1": 2, "b2": 3, "gamma": 5, "beta": 7, "fc2_1": 9}[what]
            return bias[:, first + c:first + c + 1]

        def bias_fc2(b, c):
            return bias[:, 8:9] if c == 0 else bias_of(b, "fc2_1")

        def pair(stage):
            area = AREAS[stage][0]
            if area < 2:
                return pairs[:, area]
            return (hid_ps if area == 2 else acc)[:].rearrange("p a n -> p (a n)")

        phase_of = {lt: n for n, lt in enumerate(PHASES)}
        layer3_before = {ph: sum(1 for q in range(ph) if PHASES[q][0] == 3) for ph in range(len(PHASES) + 1)}
        layer2_before = {ph: ph - n for ph, n in layer3_before.items()}
        LORA_LOADS = 16

        def plain_dest(name):
            if name == "w0":
                return w0_hi[:], w0_lo[:]
            what, n = name.split("_")
            n = int(n)
            if what == "fc1":
                return fc1_hi[:, :, n * HALF:(n + 1) * HALF], fc1_lo[:, :, n * HALF:(n + 1) * HALF]
            return fc2_hi[:, :, n * P:(n + 1) * P], fc2_lo[:, :, n * P:(n + 1) * P]

        def merged_dest(name):
            what, n = name.split("_")
            n = int(n)
            if what == "wi":
                return wi_hi[:, :, n * HALF:(n + 1) * HALF], wi_lo[:, :, n * HALF:(n + 1) * HALF]
            h = CHUNKS // 2
            return wo_hi[:, n * h:(n + 1) * h, :], wo_lo[:, n * h:(n + 1) * h, :]

        def shaped(flat, name):
            if name == "w0":
                return flat[:, 0:K * D].rearrange("p (k n) -> p k n", k=K)
            what = name[:3]
            if what in ("fc1", "wi_"):
                return flat.rearrange("p (k n) -> p k n", k=K)
            if what == "fc2":
                return flat.rearrange("p (j n) -> p j n", j=CHUNKS)
            return flat.rearrange("p (j n) -> p j n", j=CHUNKS // 2)

        def drained(pe, stage):
            if AREAS[stage][1] is None:
                return
            name, arg = AREAS[stage][1]
            if name == "bias":
                pe.wait_ge(bias_ready, arg + 1)
            elif name == "x_in":
                pe.wait_ge(x_full, K * (arg + 1))
            elif name == "w_plain":
                pe.wait_ge(plain_lo, PLAIN.index(arg) + 1)
            elif name == "l0":
                pe.wait_ge(x1_full, K * (arg + 1))
            elif name == "l1a":
                pe.wait_ge(h1_full, arg + 1)
            elif name == "l1b":
                pe.wait_ge(s_full, K * (arg + 1))
            elif name == "ln_in":
                pe.wait_ge(norm_ready, arg + 1)
            elif name == "ln_out":
                pe.wait_ge(affine_ready, K * (arg + 1))
            elif name == "lora_b_wi":
                pe.wait_ge(lb_lo, 2 * arg + 1)
            elif name == "lora_b_wo":
                pe.wait_ge(lb_lo, 2 * arg + 2)
            elif name == "w_turn":
                pe.wait_ge(turned, TURNED.index(arg) + 1)
            elif name == "w_lora":
                pe.wait_ge(summed, TURNED.index(arg) + 1)
            else:
                pe.wait_ge(out_copied, layer3_before[phase_of[(3, arg)]] + 1)

        def rows_of(table, i, first, rows):
            return rows[first:first + K, :], table[bass.ds(i, 1)].rearrange("a (r p) -> (a r) p", p=P)

        def bias_loads_first(q, lang, subj, b):
            done, rows, at = bias_loaded[b], bias_raw[b], 9 * (b == 0)
            q.dma_start(*rows_of(b0, subj, at, rows)).then_inc(done, 16)
            for first, table in ((3, b2), (5, gamma), (7, beta)):
                q.dma_start(*rows_of(table, lang, at + first, rows)).then_inc(done, 16)

        def shared_bias_loads(q, done, rows, at):
            if at:
                q.dma_start(rows[0:CHUNKS, :], fc1_b.rearrange("(r p) -> r p", p=P)).then_inc(done, 16)
                q.dma_start(rows[CHUNKS:CHUNKS + 1, :], fc2_b[0:P].rearrange("(r p) -> r p", p=P)).then_inc(done, 16)
            q.dma_start(rows[at + 9:at + 10, 0:SHARED - P],
                        fc2_b[P:SHARED].rearrange("(r p) -> r p", r=1)).then_inc(done, 16)

        def half_row_loads(q, lang, expert, b):
            done, rows, at = rest_loaded[b], bias_raw[b], 9 * (b == 0)
            for half in range(2):
                q.dma_start(rows[at + 2:at + 3, half * A:(half + 1) * A], b1[bass.ds(lang, 1)]).then_inc(done, 16)
            q.dma_start(rows[at + 9:at + 10, SHARED - P:P], ex_b[bass.ds(expert, 1)]).then_inc(done, 16)

        FIRST_LOADS, REST_LOADS = 4, [6, 4]

        def adapt_loads(q, lang, b):
            q.dma_start(w1_raw[:], w1[bass.ds(lang, 1)].rearrange("a (k p) n -> p (a k) n", p=P)).then_inc(adapt_loaded[b], 16)
            for half in range(2):
                q.dma_start(w2_raw[half * A:(half + 1) * A, :],
                            w2[bass.ds(lang, 1)].rearrange("a p n -> (a p) n")).then_inc(adapt_loaded[b], 16)

        block = ctx.enter_context(nc.Block())

        @block.sync
        def _(sp):
            def load_x(t):
                if t >= 2:
                    sp.wait_ge(pair_full, PAIR_NO[("ln_out", t - 2)] + 1)
                sp.dma_start(x_tok[:, t % 2], x_rows[t * TOKENS:(t + 1) * TOKENS, :].rearrange(
                    "(p k) d -> p k d", k=BLK)).then_inc(x_loaded[t], 16)

            def load_piece(n):
                b, name = PIECES[n]
                slot, done = raw[:, n % RAW_SLOTS], raw_loaded[n % RAW_SLOTS]
                if n >= RAW_SLOTS:
                    old = PIECES[n - RAW_SLOTS]
                    kind = "w_turn" if old in TURNED else "w_plain"
                    sp.wait_ge(pair_full, PAIR_NO[(kind, old)] + 1)
                what, _, half = name.partition("_")
                if name == "w0":
                    sp.dma_start(slot[:, 0:K * D].rearrange("p (c h) -> p c h", c=K),
                                 w0[bass.ds(subj[b], 1)].rearrange("a (c p) h -> p (a c) h", p=P)).then_inc(done, 16)
                elif what in ("fc1", "wi"):
                    source = (fc1_w if what == "fc1" else wi)[int(half) * HALF:(int(half) + 1) * HALF, :]
                    sp.dma_start(slot.rearrange("p (c h) -> p c h", c=CHUNKS // 2),
                                 source.rearrange("(c p) h -> p c h", p=P)).then_inc(done, 16)
                elif name == "fc2_0":
                    sp.dma_start(slot, fc2_w[0:P, :]).then_inc(done, 16)
                elif name == "fc2_1":
                    sp.dma_start(slot[0:SHARED - P], fc2_w[P:SHARED, :]).then_inc(done, 16)
                    sp.dma_start(slot[SHARED - P:P],
                                 ex_w[bass.ds(expert[b], 1)].rearrange("a p h -> (a p) h")).then_inc(done, 16)
                else:
                    sp.dma_start(slot.rearrange("p (c f) -> p c f", c=K),
                                 wo[:, int(half) * HALF:(int(half) + 1) * HALF].rearrange(
                                     "(c p) f -> p c f", p=P)).then_inc(done, 16)

            def load_lora(b):
                if b:
                    sp.wait_ge(la_hi, b)
                    sp.wait_ge(la_lo, b)
                    sp.wait_ge(lb_copied, 2 * b)
                own = [t[bass.ds(subj[b], 1)].rearrange("a r d -> (a r) d") for t in (ewi_a, ewo_a, ewi_b, ewo_b)]
                for rep in range(3):
                    for n, (for_wi, for_wo) in enumerate(((cwi_a, cwo_a), own[0:2])):
                        r = rep * RANK2 + n * R
                        sp.dma_start(la_raw[r:r + R, 0:D], for_wi).then_inc(lora_loaded[b], 16)
                        sp.dma_start(la_raw[r:r + R, D:D + F], for_wo).then_inc(lora_loaded[b], 16)
                for n, (for_wi, for_wo) in enumerate(((cwi_b, cwo_b), own[2:4])):
                    sp.dma_start(lb_raw[:, n, 0:CHUNKS, :],
                                   for_wi.rearrange("(p j) r -> p j r", j=CHUNKS)).then_inc(lora_loaded[b], 16)
                    sp.dma_start(lb_raw[:, n, CHUNKS:CHUNKS + K, :],
                                   for_wo.rearrange("(p j) r -> p j r", j=K)).then_inc(lora_loaded[b], 16)

            sp.dma_start(idx[0:1, 0:B], subj_idx.rearrange("(a b) -> a b", a=1)).then_inc(subj_loaded, 16)
            load_x(0)
            for n, source in ((1, lang_idx), (2, exp_idx)):
                sp.dma_start(idx[0:1, n * B:(n + 1) * B], source.rearrange("(a b) -> a b", a=1)).then_inc(idx_loaded, 16)
            load_x(1)
            sp.wait_ge(subj_loaded, 16)
            subj = [sp.value_load(idx[0:1, b:b + 1], min_val=0, max_val=w0.shape[0] - 1) for b in range(B)]
            load_piece(0)
            sp.wait_ge(idx_loaded, 32)
            lang = [sp.value_load(idx[0:1, B + b:B + b + 1], min_val=0, max_val=w1.shape[0] - 1) for b in range(B)]
            expert = [sp.value_load(idx[0:1, 2 * B + b:2 * B + b + 1], min_val=0, max_val=ex_w.shape[0] - 1)
                      for b in range(B)]
            bias_loads_first(sp, lang[0], subj[0], 0)
            load_piece(1)
            adapt_loads(sp, lang[0], 0)
            load_piece(2)
            load_piece(3)
            load_lora(0)
            bias_loads_first(sp, lang[1], subj[1], 1)
            shared_bias_loads(sp, rest_loaded[1], bias_raw[1], 0)
            half_row_loads(sp, lang[1], expert[1], 1)
            for name, arg in PLAN:
                if name in ("w_plain", "w_turn") and PIECE_NO[arg] + RAW_SLOTS < len(PIECES):
                    load_piece(PIECE_NO[arg] + RAW_SLOTS)
                elif name == "ln_out" and arg + 2 < TILES:
                    load_x(arg + 2)
                elif name == "lora_b_wi" and arg == 0:
                    sp.wait_ge(adapt_hi, 3)
                    sp.wait_ge(adapt_lo, 2)
                    adapt_loads(sp, lang[1], 1)
                    load_lora(1)
                elif name == "out":
                    n = layer3_before[phase_of[(3, arg)]]
                    sp.wait_ge(out_copied, n + 1)
                    sp.dma_start(out_rows[arg * TOKENS:(arg + 1) * TOKENS, :].rearrange("(p k) d -> p k d", k=BLK),
                                 out_tok[:]).then_inc(out_stored, 16)
            sp.wait_ge(out_stored, 16 * TILES)

        @block.tensor
        def _(pe):
            mm = nc.tensor.matmul

            def exact(dst, w_hi, w_lo, a_hi, a_lo, start, stop):
                mm(dst, w_hi, a_hi, start=start, stop=False)
                mm(dst, w_hi, a_lo, start=False, stop=False)
                return mm(dst, w_lo, a_hi, start=False, stop=stop)

            def turn(dst, source):
                return nc.tensor.transpose(dst, source, ident[0:source.shape[0], 0:source.shape[0]])

            pe.wait_ge(ident_ready, 1)
            for n in range(WARM_UP):
                turn(acc[:, 0, 0:P], ident[:])

            for stage in PLAN:
                name, arg = stage
                if name in PAIR_STAGES:
                    drained(pe, stage)
                    dst = pair(stage)
                if name == "bias":
                    pe.wait_ge(bias_loaded[arg], 16 * FIRST_LOADS)
                    pe.wait_ge(rest_loaded[arg], 16 * REST_LOADS[arg])
                    turn(dst[:, 0:bias_raw[arg].shape[0]], bias_raw[arg][:]).then_inc(pair_full, 1)
                elif name == "x_in":
                    pe.wait_ge(x_loaded[arg], 16)
                    for k in range(K):
                        for i in range(BLK):
                            last = turn(dst[:, k * TOKENS + i * P:k * TOKENS + (i + 1) * P],
                                        x_tok[:, arg % 2, i, k * P:(k + 1) * P])
                    last.then_inc(pair_full, 1)
                elif name in ("w_plain", "w_turn"):
                    b, piece = arg
                    n = PIECE_NO[arg]
                    slot = raw[:, n % RAW_SLOTS]
                    loads = sum(2 if PIECES[q][1] == "fc2_1" else 1 for q in range(n % RAW_SLOTS, n + 1, RAW_SLOTS))
                    pe.wait_ge(raw_loaded[n % RAW_SLOTS], 16 * loads)
                    view = shaped(dst, piece)
                    if piece[:3] == "fc2":
                        for j in range(CHUNKS):
                            last = turn(view[:, j, :], slot[:, j * P:(j + 1) * P])
                    elif piece[:2] == "wo":
                        for j in range(CHUNKS // 2):
                            for c in range(K):
                                last = turn(view[:, j, c * P:(c + 1) * P], slot[:, c * HALF + j * P:c * HALF + (j + 1) * P])
                    else:
                        for k in range(K):
                            for c in range(K if piece == "w0" else CHUNKS // 2):
                                last = turn(view[:, k, c * P:(c + 1) * P], slot[:, c * D + k * P:c * D + (k + 1) * P])
                    last.then_inc(pair_full, 1)
                elif name in ("lora_b_wi", "lora_b_wo"):
                    pe.wait_ge(lb_copied, 2 * (arg + 1))
                    first, n = (0, CHUNKS) if name == "lora_b_wi" else (CHUNKS, K)
                    for j in range(n):
                        last = turn(dst[0:3 * RANK2, j * P:(j + 1) * P],
                                    lb_rep[:, first + j].rearrange("p a b r -> p (a b r)"))
                    last.then_inc(pair_full, 1)
                elif name == "w_lora":
                    b, piece = arg
                    half = int(piece[3:])
                    pe.wait_ge(la_lo, b + 1)
                    pe.wait_ge(lb_lo, 2 * (b + 1))
                    if piece[:2] == "wi":
                        for k in range(K):
                            last = mm(dst[:, k * HALF:(k + 1) * HALF], la[:, k * P:(k + 1) * P],
                                      lb[:, half * HALF:(half + 1) * HALF], start=True, stop=True)
                    else:
                        for j in range(CHUNKS // 2):
                            f = D + half * HALF + j * P
                            last = mm(dst[:, j * D:(j + 1) * D], la[:, f:f + P], lb[:, F:F + D], start=True, stop=True)
                    last.then_inc(pair_full, 1)
                elif name == "l0":
                    s = arg % RES_SLOTS
                    pe.wait_ge(plain_lo, PLAIN.index((arg // PER_BATCH, "w0")) + 1)
                    for k in range(K):
                        pe.wait_ge(x_lo, K * arg + k + 1)
                        for c in range(K):
                            last = exact(dst[:, c * TOKENS:(c + 1) * TOKENS], w0_hi[:, k, c * P:(c + 1) * P],
                                         w0_lo[:, k, c * P:(c + 1) * P], res_hi[:, s, k], res_lo[:, s, k],
                                         k == 0, k == K - 1)
                    last.then_inc(pair_full, 1)
                elif name == "l1a":
                    s = arg % RES_SLOTS
                    pe.wait_ge(adapt_lo, 2 * (arg // PER_BATCH + 1))
                    for k in range(K):
                        pe.wait_ge(x1_lo, K * arg + k + 1)
                        last = exact(dst[:, 0:TOKENS], w1_hi[:, k].rearrange("p a n -> p (a n)"),
                                     w1_lo[:, k].rearrange("p a n -> p (a n)"), res_hi[:, s, k], res_lo[:, s, k],
                                     k == 0, k == K - 1)
                    last.then_inc(pair_full, 1)
                elif name == "l1b":
                    pe.wait_ge(h1_hi_s, arg + 1)
                    for c in range(K):
                        mm(dst[:, c * TOKENS:(c + 1) * TOKENS], w2_both[:, c * P:(c + 1) * P], h1_hi[:],
                           start=True, stop=False)
                    pe.wait_ge(h1_lo_s, arg + 1)
                    for c in range(K):
                        last = mm(dst[:, c * TOKENS:(c + 1) * TOKENS], w2_both[0:A, c * P:(c + 1) * P], h1_lo[:],
                                  start=False, stop=True)
                    last.then_inc(pair_full, 1)
                elif name == "ln_in":
                    pe.wait_ge(s_full, K * (arg + 1))
                    for i in range(BLK):
                        for k in range(K):
                            last = turn(dst[:, i * D + k * P:i * D + (k + 1) * P], xt[:, arg % 2, k, i * P:(i + 1) * P])
                    last.then_inc(pair_full, 1)
                elif name == "ln_out":
                    pe.wait_ge(norm_ready, arg + 1)
                    for k in range(K):
                        for i in range(BLK):
                            last = turn(dst[:, k * TOKENS + i * P:k * TOKENS + (i + 1) * P],
                                        x_tok[:, arg % 2, i, k * P:(k + 1) * P])
                    last.then_inc(pair_full, 1)
                elif name == "out":
                    pe.wait_ge(res_full, K * (phase_of[(3, arg)] + 1))
                    for i in range(BLK):
                        for k in range(K):
                            last = turn(dst[:, i * D + k * P:i * D + (k + 1) * P],
                                        res[:, arg % RES_SLOTS, k, i * P:(i + 1) * P])
                    last.then_inc(pair_full, 1)
                elif name == "up":
                    ph, j = divmod(arg, CHUNKS)
                    layer, t = PHASES[ph]
                    b = t // PER_BATCH
                    s = t % RES_SLOTS
                    if arg == 0:
                        pe.wait_ge(plain_lo, 1 + max(PLAIN.index(a) for (n, a), (area, _) in AREAS.items() if area == 2))
                    if arg >= 2 and arg - 2 in GELUS:
                        pe.wait_ge(hid_full, GELUS.index(arg - 2) + 1)
                    elif arg >= 2:
                        pe.wait_ge(hid_lo_s, arg - 1)
                    if j % (CHUNKS // 2) == 0:
                        half = j // (CHUNKS // 2)
                        if layer == 2:
                            pe.wait_ge(plain_lo, PLAIN.index((0, f"fc1_{half}")) + 1)
                        else:
                            pe.wait_ge(merged_lo, TURNED.index((b, f"wi_{half}")) + 1)
                    w_hi, w_lo = (fc1_hi, fc1_lo) if layer == 2 else (wi_hi, wi_lo)
                    for k in range(K):
                        if j == 0 and layer == 2:
                            pe.wait_ge(x2_lo, K * t + k + 1)
                        elif j == 0 and k == 0:
                            pe.wait_ge(x3_lo, layer2_before[phase_of[(2, t)]] + 1)
                        last = exact(hid_ps[:, arg % 2], w_hi[:, k, j * P:(j + 1) * P], w_lo[:, k, j * P:(j + 1) * P],
                                     res_hi[:, s, k], res_lo[:, s, k], k == 0, k == K - 1)
                    last.then_inc(up_done, 1)
                elif name == "down":
                    ph, j = divmod(arg, CHUNKS)
                    layer, t = PHASES[ph]
                    b = t // PER_BATCH
                    if layer == 2:
                        if j == 0:
                            pe.wait_ge(plain_lo, PLAIN.index((b, "fc2_1")) + 1)
                        w_hi, w_lo = fc2_hi, fc2_lo
                    else:
                        if j % (CHUNKS // 2) == 0:
                            pe.wait_ge(merged_lo, TURNED.index((b, f"wo_{j // (CHUNKS // 2)}")) + 1)
                        w_hi, w_lo = wo_hi, wo_lo
                    pe.wait_ge(hid_lo_s, arg + 1)
                    for c in range(K):
                        if j == 0 and ph:
                            pe.wait_ge(res_full, K * (ph - 1) + c + 1)
                        last = exact(acc[:, c], w_hi[:, j, c * P:(c + 1) * P], w_lo[:, j, c * P:(c + 1) * P],
                                     hid_hi[:, arg % HID_SLOTS], hid_lo[:, arg % HID_SLOTS], j == 0, j == CHUNKS - 1)
                        if j == CHUNKS - 1 and c < K - 1:
                            last.then_inc(acc_full, 1)
                    last.then_inc(down_done, 1)

        @block.scalar
        def _(act):
            fn = nc.scalar.activation

            act.wait_ge(mhalf_ready, 1)
            fn(table_warm[:], mhalf[:, 0:1], ACT.Gelu)

            for stage in PLAN:
                name, arg = stage
                if name in PAIR_STAGES and name not in ("w_plain", "l0", "l1a", "l1b", "ln_in", "w_lora"):
                    source = pair(stage)
                    act.wait_ge(pair_full, PAIR_NO[stage] + 1)
                if name == "bias":
                    first, n = (0, 19) if arg == 0 else (19, 10)
                    fn(bias[:, first:first + n], source[:, 0:n], ACT.Copy).then_inc(bias_ready, 1)
                elif name == "x_in":
                    s = arg % RES_SLOTS
                    if arg >= RES_SLOTS:
                        act.wait_ge(pair_full, PAIR_NO[("out", arg - RES_SLOTS)] + 1)
                    if arg >= 2:
                        act.wait_ge(x2_full, K * (arg - 1))
                    for k in range(K):
                        ps = source[:, k * TOKENS:(k + 1) * TOKENS]
                        fn(res_hi[:, s, k], ps, ACT.Copy).then_inc(x_hi, 1)
                        fn(xt[:, arg % 2, k], ps, ACT.Copy).then_inc(x_full, 1)
                elif name == "w_hi":
                    b, piece = arg
                    source = pair(("w_plain", arg))
                    act.wait_ge(pair_full, PAIR_NO[("w_plain", arg)] + 1)
                    if piece == "w0" and b:
                        act.wait_ge(pair_full, PAIR_NO[("l0", b * PER_BATCH - 1)] + 1)
                    if piece == "fc2_1" and b:
                        act.wait_ge(down_done, CHUNKS * (phase_of[(2, b * PER_BATCH - 1)] + 1))
                    fn(plain_dest(piece)[0], shaped(source, piece), ACT.Copy).then_inc(plain_hi, 1)
                elif name == "w_adapt":
                    act.wait_ge(adapt_loaded[arg], 48)
                    if arg:
                        act.wait_ge(pair_full, PAIR_NO[("l1b", arg * PER_BATCH - 1)] + 1)
                    for half in range(2):
                        fn(w1_hi[:, :, half], w1_raw[:], ACT.Copy).then_inc(adapt_hi, 1)
                    fn(w2_both[:], w2_raw[:], ACT.Copy).then_inc(adapt_hi, 1)
                elif name == "x1_hi":
                    s = arg % RES_SLOTS
                    act.wait_ge(pair_full, PAIR_NO[("l0", arg)] + 1)
                    for k in range(K):
                        act.wait_ge(x1_full, K * arg + k + 1)
                        fn(res_hi[:, s, k], res[:, s, k], ACT.Copy).then_inc(x1_hi, 1)
                elif name == "h1":
                    b = arg // PER_BATCH
                    source = pair(("l1a", arg))
                    act.wait_ge(pair_full, PAIR_NO[("l1a", arg)] + 1)
                    if arg:
                        act.wait_ge(pair_full, PAIR_NO[("l1b", arg - 1)] + 1)
                    fn(h1_hi[:], source[:, 0:TOKENS], ACT.Relu, bias=bias_of(b, "b1")).then_inc(h1_hi_s, 1)
                    fn(h1[:], source[0:A, 0:TOKENS], ACT.Relu, bias=bias_of(b, "b1")[0:A]).then_inc(h1_full, 1)
                elif name == "ln_out":
                    b = arg // PER_BATCH
                    for k in range(K):
                        fn(xt[:, arg % 2, k], source[:, k * TOKENS:(k + 1) * TOKENS], ACT.Identity,
                           bias=bias_of(b, "beta", k), scale=bias_of(b, "gamma", k)).then_inc(affine_ready, 1)
                elif name == "x2_hi":
                    s = arg % RES_SLOTS
                    for k in range(K):
                        act.wait_ge(x2_full, K * arg + k + 1)
                        fn(res_hi[:, s, k], res[:, s, k], ACT.Copy).then_inc(x2_hi, 1)
                elif name == "lora_a":
                    act.wait_ge(lora_loaded[arg], 16 * LORA_LOADS)
                    if arg:
                        act.wait_ge(pair_full, PAIR_NO[("w_lora", (arg - 1, "wo_1"))] + 1)
                    fn(la[:], la_raw[:], ACT.Copy).then_inc(la_hi, 1)
                elif name in ("lora_b_wi", "lora_b_wo"):
                    first, n, at = (0, CHUNKS, 0) if name == "lora_b_wi" else (CHUNKS, K, F)
                    fn(lb[:, at:at + n * P].rearrange("r (p j) -> r j p", j=n),
                       source[0:3 * RANK2, 0:n * P].rearrange("r (j p) -> r j p", j=n), ACT.Copy,
                       scale=ALPHA).then_inc(lb_hi, 1)
                elif name == "w_turn":
                    n = TURNED.index(arg)
                    if n >= 2:
                        act.wait_ge(merged_lo, n - 1)
                    fn(merged[:, n % 2], source, ACT.Copy).then_inc(turned, 1)
                elif name == "w_split":
                    b, piece = arg
                    n = TURNED.index(arg)
                    act.wait_ge(summed, n + 1)
                    if b:
                        ph = phase_of[(3, b * PER_BATCH - 1)]
                        used = CHUNKS * ph + CHUNKS // 2 * (int(piece[3:]) + 1)
                        act.wait_ge(up_done if piece[:2] == "wi" else down_done, used)
                    fn(merged_dest(piece)[0], shaped(merged[:, n % 2], piece), ACT.Copy).then_inc(merged_hi, 1)
                elif name == "up":
                    ph, j = divmod(arg, CHUNKS)
                    layer, t = PHASES[ph]
                    act.wait_ge(up_done, arg + 1)
                    if arg >= HID_SLOTS:
                        act.wait_ge(down_done, arg - HID_SLOTS + 1)
                    dst = hid_hi[:, arg % HID_SLOTS]
                    if layer == 2:
                        n = GELUS.index(arg)
                        fn(dst, hid_ps[:, arg % 2], ACT.Gelu, bias=bias_fc1(j)).then_inc(hid_hi_s, 1)
                        if n >= 2:
                            act.wait_ge(hid_lo_s, GELUS[n - 2] + 1)
                        fn(hid[:, n % 2], hid_ps[:, arg % 2], ACT.Gelu, bias=bias_fc1(j)).then_inc(hid_full, 1)
                    else:
                        fn(dst, hid_ps[:, arg % 2], ACT.Relu).then_inc(hid_hi_s, 1)
                elif name == "res":
                    layer, t = PHASES[arg]
                    if layer == 2:
                        act.wait_ge(res_full, K * (arg + 1))
                        fn(res_hi[:, t % RES_SLOTS], res[:, t % RES_SLOTS], ACT.Copy).then_inc(x3_hi, 1)
                elif name == "out":
                    n = layer3_before[phase_of[(3, arg)]]
                    if n:
                        act.wait_ge(out_stored, 16 * n)
                    fn(out_tok[:].rearrange("p k d -> p (k d)"), source, ACT.Copy).then_inc(out_copied, 1)

        @block.vector
        def _(dve):
            v = nc.vector

            def subtract_high(lo, whole, hi):
                return v.tensor_tensor(lo, whole, hi.bitcast(F32), ALU.subtract)

            for stage in PLAN:
                name, arg = stage
                if name in PAIR_STAGES:
                    source = pair(stage)
                if name == "w_lo":
                    source = pair(("w_plain", arg))
                    dve.wait_ge(plain_hi, PLAIN.index(arg) + 1)
                    hi, lo = plain_dest(arg[1])
                    subtract_high(lo, shaped(source, arg[1]), hi).then_inc(plain_lo, 1)
                elif name == "w_adapt":
                    dve.wait_ge(adapt_hi, 3 * (arg + 1))
                    for half in range(2):
                        last = subtract_high(w1_lo[:, :, half], w1_raw[:], w1_hi[:, :, half])
                    last.then_inc(adapt_lo, 1)
                    subtract_high(w2_both[A:2 * A], w2_raw[A:2 * A], w2_both[A:2 * A]).then_inc(adapt_lo, 1)
                elif name == "x_in_lo":
                    s = arg % RES_SLOTS
                    for k in range(K):
                        dve.wait_ge(x_full, K * arg + k + 1)
                        subtract_high(res_lo[:, s, k], xt[:, arg % 2, k], res_hi[:, s, k]).then_inc(x_lo, 1)
                elif name == "x1":
                    b, s = arg // PER_BATCH, arg % RES_SLOTS
                    source = pair(("l0", arg))
                    dve.wait_ge(pair_full, PAIR_NO[("l0", arg)] + 1)
                    dve.wait_ge(bias_ready, b + 1)
                    for k in range(K):
                        v.scalar_tensor_tensor(out=res[:, s, k], in0=source[:, k * TOKENS:(k + 1) * TOKENS],
                                               scalar=bias_of(b, "b0", k), in1=xt[:, arg % 2, k], op0=ALU.add,
                                               op1=ALU.add).then_inc(x1_full, 1)
                elif name == "x1_lo":
                    s = arg % RES_SLOTS
                    for k in range(K):
                        dve.wait_ge(x1_hi, K * arg + k + 1)
                        subtract_high(res_lo[:, s, k], res[:, s, k], res_hi[:, s, k]).then_inc(x1_lo, 1)
                elif name == "h1_lo":
                    dve.wait_ge(h1_full, arg + 1)
                    subtract_high(h1_lo[:], h1[:], h1_hi[0:A]).then_inc(h1_lo_s, 1)
                elif name == "s":
                    b, s = arg // PER_BATCH, arg % RES_SLOTS
                    source = pair(("l1b", arg))
                    dve.wait_ge(pair_full, PAIR_NO[("l1b", arg)] + 1)
                    for k in range(K):
                        v.scalar_tensor_tensor(out=xt[:, arg % 2, k], in0=source[:, k * TOKENS:(k + 1) * TOKENS],
                                               scalar=bias_of(b, "b2", k), in1=res[:, s, k], op0=ALU.add,
                                               op1=ALU.add).then_inc(s_full, 1)
                elif name == "ln_in":
                    dve.wait_ge(pair_full, PAIR_NO[stage] + 1)
                    if arg:
                        dve.wait_ge(rstd_ready, arg)
                    done = (2 * BLK + 1) * arg
                    for i in range(BLK):
                        v.bn_stats(stats[:, i, :], source[:, i * D:(i + 1) * D]).then_inc(stat_step, 1)
                    dve.wait_ge(stat_step, done + BLK)
                    for i in range(BLK):
                        v.bn_aggr(mv[:, i, :], stats[:, i, :]).then_inc(stat_step, 1)
                    dve.wait_ge(stat_step, done + 2 * BLK)
                    v.tensor_scalar(var_eps[:], mv[:, :, 1], LN_EPS, None, ALU.add).then_inc(stat_step, 1)
                elif name == "ln_norm":
                    dve.wait_ge(rstd_ready, arg + 1)
                    ps = pair(("ln_in", arg))
                    for i in range(BLK):
                        last = v.tensor_scalar(x_tok[:, arg % 2, i, :], ps[:, i * D:(i + 1) * D], mv[:, i, 0:1],
                                               rstd[:, i:i + 1], ALU.subtract, ALU.mult)
                    last.then_inc(norm_ready, 1)
                elif name == "x2":
                    s = arg % RES_SLOTS
                    for k in range(K):
                        dve.wait_ge(affine_ready, K * arg + k + 1)
                        v.tensor_tensor(res[:, s, k], xt[:, arg % 2, k], res[:, s, k], ALU.add).then_inc(x2_full, 1)
                elif name == "x2_lo":
                    s = arg % RES_SLOTS
                    for k in range(K):
                        dve.wait_ge(x2_hi, K * arg + k + 1)
                        subtract_high(res_lo[:, s, k], res[:, s, k], res_hi[:, s, k]).then_inc(x2_lo, 1)
                elif name == "lora_a":
                    dve.wait_ge(la_hi, arg + 1)
                    low = slice(2 * RANK2, 3 * RANK2)
                    subtract_high(la[low], la_raw[low], la[low]).then_inc(la_lo, 1)
                    if arg:
                        dve.wait_ge(pair_full, PAIR_NO[("lora_b_wo", arg - 1)] + 1)
                    for n in range(2):
                        v.tensor_copy(lb_rep[:, :, :, n, :],
                                      lb_raw[:, n].unsqueeze(2).to_broadcast([P, CHUNKS + K, 3, R])).then_inc(lb_copied, 1)
                elif name in ("lora_b_wi", "lora_b_wo"):
                    dve.wait_ge(lb_hi, 2 * arg + (name == "lora_b_wo") + 1)
                    first, n, at = (0, CHUNKS, 0) if name == "lora_b_wi" else (CHUNKS, K, F)
                    view = lb[RANK2:2 * RANK2, at:at + n * P].rearrange("r (p j) -> r j p", j=n)
                    v.scalar_tensor_tensor(out=view, in0=source[RANK2:2 * RANK2, 0:n * P].rearrange("r (j p) -> r j p", j=n),
                                           scalar=ALPHA, in1=view.bitcast(F32), op0=ALU.mult,
                                           op1=ALU.subtract).then_inc(lb_lo, 1)
                elif name == "w_lora":
                    n = TURNED.index(arg)
                    dve.wait_ge(pair_full, PAIR_NO[stage] + 1)
                    dve.wait_ge(turned, n + 1)
                    v.tensor_tensor(merged[:, n % 2], source, merged[:, n % 2], ALU.add).then_inc(summed, 1)
                elif name == "hid_lo":
                    s = arg % HID_SLOTS
                    if arg in GELUS:
                        n = GELUS.index(arg)
                        dve.wait_ge(hid_full, n + 1)
                        subtract_high(hid_lo[:, s], hid[:, n % 2], hid_hi[:, s]).then_inc(hid_lo_s, 1)
                    else:
                        dve.wait_ge(hid_hi_s, arg + 1)
                        v.scalar_tensor_tensor(out=hid_lo[:, s], in0=hid_ps[:, arg % 2], scalar=0.0,
                                               in1=hid_hi[:, s].bitcast(F32), op0=ALU.max,
                                               op1=ALU.subtract).then_inc(hid_lo_s, 1)
                elif name == "res":
                    layer, t = PHASES[arg]
                    s, b = t % RES_SLOTS, t // PER_BATCH
                    for c in range(K):
                        if c < K - 1:
                            dve.wait_ge(acc_full, arg + 1)
                        else:
                            dve.wait_ge(down_done, CHUNKS * (arg + 1))
                        if layer == 2:
                            v.scalar_tensor_tensor(out=res[:, s, c], in0=acc[:, c], scalar=bias_fc2(b, c),
                                                   in1=res[:, s, c], op0=ALU.add, op1=ALU.add).then_inc(res_full, 1)
                        else:
                            v.tensor_tensor(res[:, s, c], acc[:, c], res[:, s, c], ALU.add).then_inc(res_full, 1)
                elif name == "res_lo":
                    layer, t = PHASES[arg]
                    if layer == 2:
                        dve.wait_ge(x3_hi, layer2_before[arg] + 1)
                        s = t % RES_SLOTS
                        subtract_high(res_lo[:, s], res[:, s], res_hi[:, s]).then_inc(x3_lo, 1)

        @block.gpsimd
        def _(pool):
            g = nc.gpsimd
            g.memset(ident[:], 0.0).then_inc(ident_zero, 1)
            g.memset(mhalf[:], -0.5).then_inc(mhalf_ready, 1)
            pool.wait_ge(ident_zero, 1)
            g.affine_select(out=ident[:], in_=ident[:], compare_op=ALU.not_equal, fill=1.0, base=0,
                            pattern=[[-1, P]], channel_multiplier=1).then_inc(ident_ready, 1)
            pool.wait_ge(mhalf_ready, 1)
            shared_bias_loads(pool, rest_loaded[0], bias_raw[0], 9)
            pool.wait_ge(idx_loaded, 32)
            lang, expert = (pool.value_load(idx[0:1, n * B:n * B + 1], min_val=0, max_val=table.shape[0] - 1)
                            for n, table in ((1, w1), (2, ex_w)))
            half_row_loads(pool, lang, expert, 0)
            for name, arg in PLAN:
                if name == "ln_in":
                    pool.wait_ge(stat_step, (2 * BLK + 1) * (arg + 1))
                    if arg:
                        pool.wait_ge(norm_ready, arg)
                    g.tensor_tensor(rstd[:], var_eps[:], mhalf[:], ALU.pow).then_inc(rstd_ready, 1)
                elif name == "w_split":
                    n = TURNED.index(arg)
                    pool.wait_ge(merged_hi, n + 1)
                    hi, lo = merged_dest(arg[1])
                    g.tensor_tensor(lo, shaped(merged[:, n % 2], arg[1]), hi.bitcast(F32), ALU.subtract).then_inc(merged_lo, 1)


_INS = ['x', 'itok_B_0_7', 'itok_B_0_8', 'itok_B_0_15', 'L0_cond_weight', 'L0_cond_bias', 'L1_cond_W1', 'L1_cond_b1',
        'L1_cond_W2', 'L1_cond_b2', 'L1_cond_gamma', 'L1_cond_beta', 'L2_cond_fc1_w', 'L2_cond_fc1_b',
        'L2_cond_fc2_w', 'L2_cond_fc2_b', 'L2_cond_experts_w', 'L2_cond_experts_b', 'L3_cond_wi', 'L3_cond_wo',
        'L3_cond_common_wi_a', 'L3_cond_common_wi_b', 'L3_cond_common_wo_a', 'L3_cond_common_wo_b',
        'L3_cond_experts_wi_a', 'L3_cond_experts_wi_b', 'L3_cond_experts_wo_a', 'L3_cond_experts_wo_b']


def kernel(**inputs):
    import numpy as _np
    import concourse.bacc as _bacc
    from concourse import mybir as _mybir
    from concourse.bass_utils import run_bass_kernel_spmd as _run

    nc = _bacc.Bacc("TRN2", target_bir_lowering=False, num_devices=1)
    arrays, args = {}, []
    for name in _INS:
        a = _np.ascontiguousarray(inputs[name])
        arrays[f"in_{name}_dram"] = a
        args.append(nc.dram_tensor(f"in_{name}_dram", a.shape, _mybir.dt.from_np(a.dtype), kind="ExternalInput").ap())
    args.append(nc.dram_tensor("out_0_dram", inputs["x"].shape, _mybir.dt.float32, kind="ExternalOutput").ap())
    build(nc, *args)
    r = _run(nc, [arrays], core_ids=[0])
    return r.results[0]["out_0_dram"]
```

```python
from contextlib import ExitStack

import concourse.bass as bass
from concourse import mybir

ALU = mybir.AluOpType
ACT = mybir.ActivationFunctionType
F32 = mybir.dt.float32
F32R = mybir.dt.float32r
I32 = mybir.dt.int32

P = 128
ALPHA = 2.0
LN_EPS = 1e-5
RAW_SLOTS = 5
LOADS_AHEAD = 4
RES_SLOTS = 3
HID_SLOTS = 3
WARM_UP = 7
KEEP_WARM = 4
RANK2 = 32

PHASES = [(2, 0), (2, 1), (3, 0), (2, 2), (3, 1), (2, 3), (3, 2), (3, 3)]
CHUNKS = 8
LAG = 2


def make_plan():
    w0_, fc1_0, fc1_1, fc2_0, fc2_1 = ((0, piece) for piece in ("w0", "fc1_0", "fc1_1", "fc2_0", "fc2_1"))
    plan = [("x_in", 0), ("w_plain", w0_), ("x_in_lo", 0), ("w_hi", w0_), ("w_lo", w0_), ("x_copy", 0),
            ("x_in", 1), ("b0", 0), ("l0", 0), ("x_in_lo", 1), ("x_copy", 1), ("w_adapt", 0), ("l0", 1),
            ("x1", 0), ("x1_hi", 0), ("bias", 0), ("x1_lo", 0), ("l1a", 0), ("x1", 1),
            ("h1", 0), ("w_plain", fc1_0), ("h1_lo", 0), ("l1b", 0), ("w_plain", fc1_1), ("x1_hi", 1),
            ("w_hi", fc1_0), ("w_lo", fc1_0), ("s", 0), ("ln_in", 0), ("w_hi", fc1_1), ("w_plain", fc2_0),
            ("w_turn", (0, "wi_0")), ("w_plain", fc2_1), ("w_lo", fc1_1), ("w_hi", fc2_0), ("w_lo", fc2_0),
            ("ln_norm", 0), ("x1_lo", 1), ("x2_base", 0), ("ln_out", 0), ("x2", 0), ("x2_hi", 0), ("x2_lo", 0),
            ("w_hi", fc2_1), ("w_lo", fc2_1), ("l1a", 1), ("w_turn", (0, "wi_1"))]
    extra = {}

    def put(at, name, arg):
        extra.setdefault(at, []).append((name, arg))

    def put_front(tile, first):
        for name, at in (("x_in", 0), ("x_in_lo", 0), ("x_copy", 0), ("l0", 2), ("x1", 2), ("x1_hi", 3),
                         ("x1_lo", 4), ("l1a", 5), ("h1", 5), ("h1_lo", 6), ("l1b", 6), ("s", 6), ("ln_in", 7),
                         ("ln_norm", 8), ("x2_base", 8), ("ln_out", 9), ("x2", 10), ("x2_hi", 11), ("x2_lo", 12)):
            put(first + at, name, tile)

    def put_merged(batch, first, step):
        for n, piece in enumerate(("wi_0", "wi_1", "wo_0", "wo_1")):
            put(first + step * n, "w_lora", (batch, piece))
            put(first + step * n + 1, "w_split", (batch, piece))

    for at, name in ((0, "h1"), (0, "h1_lo"), (2, "l1b"), (2, "s"), (3, "ln_in"), (4, "ln_norm"), (4, "x2_base"),
                     (5, "ln_out"), (5, "x2"), (6, "x2_hi"), (7, "x2_lo")):
        put(at, name, 1)
    put(5, "lora_a", 0)
    put(6, "b0", 1)
    put(7, "bias", 1)
    put(8, "lora_b_wi", 0)
    put(9, "lora_b_wo", 0)
    for at, piece in ((7, "wo_0"), (8, "wo_1")):
        put(at, "w_turn", (0, piece))
    put_merged(0, 11, 1)
    for at, piece in ((5, "w0"), (18, "fc2_1")):
        put(at, "w_plain", (1, piece))
        put(at, "w_hi", (1, piece))
        put(at + 1, "w_lo", (1, piece))
    put(9, "w_adapt", 1)
    put_front(2, 11)
    put_front(3, 27)
    put(25, "lora_a", 1)
    put(31, "lora_b_wi", 1)
    put(33, "lora_b_wo", 1)
    put_merged(1, 41, 2)
    for ph, (layer, tile) in enumerate(PHASES):
        if layer == 3:
            put(CHUNKS * ph + CHUNKS + LAG, "out", tile)
    total = CHUNKS * len(PHASES)
    for g in range(total + LAG + 2):
        if g < total:
            plan.append(("up", g))
        if 1 <= g <= total:
            plan.append(("hid_lo", g - 1))
        if g >= LAG + 1 and (g - LAG - 1) % CHUNKS == CHUNKS - 1:
            plan.append(("res_lo", (g - LAG - 1) // CHUNKS))
        plan += extra.get(g, [])
        if LAG <= g < total + LAG:
            plan.append(("down", g - LAG))
            if (g - LAG) % CHUNKS == CHUNKS - 1:
                plan.append(("res", (g - LAG) // CHUNKS))
    return plan


PLAN = make_plan()
PAIR_STAGES = ("b0", "bias", "x_in", "w_plain", "l0", "l1a", "l1b", "ln_in", "ln_out", "lora_b_wi", "lora_b_wo",
               "w_turn", "w_lora", "out")
PAIR_NO = {stage: n for n, stage in enumerate(s for s in PLAN if s[0] in PAIR_STAGES)}
HALF_NO = {stage: n for n, stage in enumerate(s for s in PLAN if s[0] in ("x_in", "l0", "l1b", "ln_in", "out"))}
FIRST_UP = PLAN.index(("up", 0))


def make_areas():
    areas, last, count = {}, {}, [0, 0]
    for stage in PAIR_NO:
        early = (stage[0] in ("w_plain", "b0", "bias") or stage == ("l0", 0)) and PLAN.index(stage) < FIRST_UP
        area = 2 * early + count[early] % 2
        if stage != ("w_turn", (0, "wi_0")):
            count[early] += 1
        areas[stage] = (area, last.get(area))
        last[area] = stage
    return areas


AREAS = make_areas()
GELUS = [g for g in range(CHUNKS * len(PHASES)) if PHASES[g // CHUNKS][0] == 2]
PIECES = [arg for name, arg in PLAN if name in ("w_plain", "w_turn")]
PIECE_NO = {arg: n for n, arg in enumerate(PIECES)}
PLAIN = [arg for name, arg in PLAN if name == "w_plain"]
TURNED = [arg for name, arg in PLAN if name == "w_turn"]
MERGED = [arg for name, arg in PLAN if name == "w_lora"]
SLOT = {(0, piece): n % (RAW_SLOTS - 1)
        for n, piece in enumerate(("w0", "fc1_0", "fc1_1", "fc2_0", "fc2_1", "wi_0", "wi_1", "wo_0", "wo_1"))}
SLOT |= {arg: RAW_SLOTS - 1 for arg in PIECES if arg[0]}
SLOT_BEFORE = {arg: ([a for a in PIECES[:n] if SLOT[a] == SLOT[arg]] or [None])[-1] for n, arg in enumerate(PIECES)}
BY_POOL = [(0, piece) for piece in ("fc1_0", "fc1_1", "fc2_0", "fc2_1")]
BY_DVE = [arg for arg in PLAIN if arg not in BY_POOL]


def build(nc, x, subj_idx, lang_idx, exp_idx, w0, b0, w1, b1, w2, b2, gamma, beta, fc1_w, fc1_b, fc2_w, fc2_b,
          ex_w, ex_b, wi, wo, cwi_a, cwi_b, cwo_a, cwo_b, ewi_a, ewi_b, ewo_a, ewo_b, out):
    B, S, D = x.shape
    F = fc1_w.shape[0]
    A = w1.shape[2]
    SHARED = fc2_w.shape[0]
    R = cwi_a.shape[0]
    K = D // P
    TOKENS = 512
    TILES = B * S // TOKENS
    BLK = TOKENS // P
    HALF = F // 2
    assert K == 2 and F == CHUNKS * P and 2 * A == P and D - SHARED == A and 2 * R == RANK2 and TILES == 4
    PER_BATCH = TILES // B
    x_rows = x.rearrange("b s d -> (b s) d")
    out_rows = out.rearrange("b s d -> (b s) d")
    n_pieces = len(PIECES)

    with ExitStack() as ctx:
        def sb(name, shape, dt=F32):
            return ctx.enter_context(nc.sbuf_tensor(name, shape, dt))

        def sem(name):
            return ctx.enter_context(nc.semaphore(name))

        w0_hi, w0_lo = (sb(f"w0_{n}", [P, K, D], F32R) for n in ("hi", "lo"))
        w1_hi, w1_lo = (sb(f"w1_{n}", [P, K, 2, A], F32R) for n in ("hi", "lo"))
        w2_both = sb("w2_both", [P, D], F32R)
        fc1_hi, fc1_lo = (sb(f"fc1_{n}", [P, K, F], F32R) for n in ("hi", "lo"))
        fc2_hi, fc2_lo = (sb(f"fc2_{n}", [P, CHUNKS, D], F32R) for n in ("hi", "lo"))
        wi_hi, wi_lo = (sb(f"wi_{n}", [P, K, F], F32R) for n in ("hi", "lo"))
        wo_hi, wo_lo = (sb(f"wo_{n}", [P, CHUNKS, D], F32R) for n in ("hi", "lo"))
        raw = sb("raw", [P, RAW_SLOTS, 1024])
        w1_raw = sb("w1_raw", [P, K, A])
        w2_raw = sb("w2_raw", [P, D])
        merged = sb("merged", [P, 2, 1024])
        la_raw = sb("la_raw", [3 * RANK2, D + F])
        la = sb("la", [3 * RANK2, D + F], F32R)
        lb_raw = sb("lb_raw", [P, 2, CHUNKS + K, R])
        lb_rep = sb("lb_rep", [P, CHUNKS + K, 3, 2, R])
        lb = sb("lb", [3 * RANK2, F + D], F32R)
        b0_raw = sb("b0_raw", [K, B, P])
        bias_raw = [sb(f"bias_raw{b}", [8 + 9 * (b == 0), P]) for b in range(B)]
        bias = sb("bias", [P, 9 + 10 * B])
        idx = sb("idx", [1, 3 * B], I32)
        ident = sb("ident", [P, P])
        mhalf = sb("mhalf", [P, BLK])
        table_warm = sb("table_warm", [P, 1])
        x_tok = sb("x_tok", [P, 2, BLK, D])
        xt = sb("xt", [P, 2, K, TOKENS])
        h1 = sb("h1", [A, TOKENS])
        h1_hi = sb("h1_hi", [P, TOKENS], F32R)
        h1_lo = sb("h1_lo", [A, TOKENS], F32R)
        stats = sb("stats", [P, BLK, 6])
        mv = sb("mv", [P, BLK, 2])
        var_eps = sb("var_eps", [P, BLK])
        rstd = sb("rstd", [P, BLK])
        shift = sb("shift", [P, BLK])
        res = sb("res", [P, RES_SLOTS, K, TOKENS])
        res_hi, res_lo = (sb(f"res_{n}", [P, RES_SLOTS, K, TOKENS], F32R) for n in ("hi", "lo"))
        hid = sb("hid", [P, 2, TOKENS])
        hid_hi, hid_lo = (sb(f"hid_{n}", [P, HID_SLOTS, TOKENS], F32R) for n in ("hi", "lo"))
        out_tok = sb("out_tok", [P, BLK, D])

        pairs = ctx.enter_context(nc.psum_tensor("pairs", [P, 2, 1024], F32))
        hid_ps = ctx.enter_context(nc.psum_tensor("hid_ps", [P, 2, TOKENS], F32))
        acc = ctx.enter_context(nc.psum_tensor("acc", [P, K, TOKENS], F32))

        subj_loaded = sem("subj_loaded")
        idx_loaded = sem("idx_loaded")
        x_loaded = [sem(f"x_loaded{t}") for t in range(TILES)]
        raw_loaded = [sem(f"raw_loaded{r}") for r in range(RAW_SLOTS)]
        bias_loaded = [sem(f"bias_loaded{b}") for b in range(B)]
        b0_loaded = [sem(f"b0_loaded{b}") for b in range(B)]
        rest_loaded = [sem(f"rest_loaded{b}") for b in range(B)]
        adapt_loaded = [sem(f"adapt_loaded{b}") for b in range(B)]
        lora_loaded = [sem(f"lora_loaded{b}") for b in range(B)]
        out_stored = sem("out_stored")
        pair_full = sem("pair_full")
        half_full = sem("half_full")
        up_done = sem("up_done")
        down_done = sem("down_done")
        acc_full = sem("acc_full")
        ident_zero = sem("ident_zero")
        ident_ready = sem("ident_ready")
        mhalf_ready = sem("mhalf_ready")
        b0_ready = sem("b0_ready")
        bias_ready = sem("bias_ready")
        plain_hi, plain_lo = sem("plain_hi"), sem("plain_lo")
        plain_copied, pool_lo = sem("plain_copied"), sem("pool_lo")
        adapt_hi, adapt_lo = sem("adapt_hi"), sem("adapt_lo")
        turned = sem("turned")
        summed = sem("summed")
        merged_hi, merged_lo = sem("merged_hi"), sem("merged_lo")
        la_hi, la_lo = sem("la_hi"), sem("la_lo")
        lb_copied = sem("lb_copied")
        lb_hi, lb_lo = sem("lb_hi"), sem("lb_lo")
        x_hi, x_lo = sem("x_hi"), sem("x_lo")
        x_full = sem("x_full")
        x1_full = sem("x1_full")
        x1_hi, x1_lo = sem("x1_hi"), sem("x1_lo")
        h1_full, h1_hi_s, h1_lo_s = sem("h1_full"), sem("h1_hi_s"), sem("h1_lo_s")
        s_full = sem("s_full")
        stat_step = sem("stat_step")
        rstd_ready = sem("rstd_ready")
        shift_ready = sem("shift_ready")
        norm_dve, norm_act = sem("norm_dve"), sem("norm_act")
        base_ready = sem("base_ready")
        x2_full, x2_hi, x2_lo = sem("x2_full"), sem("x2_hi"), sem("x2_lo")
        hid_full = sem("hid_full")
        hid_hi_s, hid_lo_s = sem("hid_hi_s"), sem("hid_lo_s")
        res_full = sem("res_full")
        x3_hi, x3_lo = sem("x3_hi"), sem("x3_lo")
        out_copied = sem("out_copied")

        def bias_fc1(j):
            return bias[:, j:j + 1]

        def bias_of(b, what, c=0, n=1):
            first = 9 + 10 * b + {"b1": 0, "b2": 1, "gamma": 3, "beta": 5, "fc2_1": 7, "b0": 8}[what]
            return bias[:, first + c:first + c + n]

        def bias_fc2(b, c):
            return bias[:, 8:9] if c == 0 else bias_of(b, "fc2_1")

        def pair(stage):
            area = AREAS[stage][0]
            if area < 2:
                return pairs[:, area]
            return (hid_ps if area == 2 else acc)[:].rearrange("p a n -> p (a n)")

        phase_of = {lt: n for n, lt in enumerate(PHASES)}
        layer3_before = {ph: sum(1 for q in range(ph) if PHASES[q][0] == 3) for ph in range(len(PHASES) + 1)}
        layer2_before = {ph: ph - n for ph, n in layer3_before.items()}
        LORA_LOADS = 16

        def plain_dest(name):
            if name == "w0":
                return w0_hi[:], w0_lo[:]
            what, n = name.split("_")
            n = int(n)
            if what == "fc1":
                return fc1_hi[:, :, n * HALF:(n + 1) * HALF], fc1_lo[:, :, n * HALF:(n + 1) * HALF]
            return fc2_hi[:, :, n * P:(n + 1) * P], fc2_lo[:, :, n * P:(n + 1) * P]

        def merged_dest(name):
            what, n = name.split("_")
            n = int(n)
            if what == "wi":
                return wi_hi[:, :, n * HALF:(n + 1) * HALF], wi_lo[:, :, n * HALF:(n + 1) * HALF]
            h = CHUNKS // 2
            return wo_hi[:, n * h:(n + 1) * h, :], wo_lo[:, n * h:(n + 1) * h, :]

        def shaped(flat, name):
            if name == "w0":
                return flat[:, 0:K * D].rearrange("p (k n) -> p k n", k=K)
            what = name[:3]
            if what in ("fc1", "wi_"):
                return flat.rearrange("p (k n) -> p k n", k=K)
            if what == "fc2":
                return flat.rearrange("p (j n) -> p j n", j=CHUNKS)
            return flat.rearrange("p (j n) -> p j n", j=CHUNKS // 2)

        def wait_bank(engine, stage, half):
            if half == 0:
                engine.wait_ge(half_full, HALF_NO[stage] + 1)
            else:
                engine.wait_ge(pair_full, PAIR_NO[stage] + 1)

        def wait_norm(engine, t, block):
            half = BLK // 2
            engine.wait_ge(norm_dve, half * t + min(block + 1, half))
            if block >= half:
                engine.wait_ge(norm_act, half * t + block - half + 1)

        def wait_plain(pe, piece):
            if piece in BY_POOL:
                pe.wait_ge(pool_lo, BY_POOL.index(piece) + 1)
            else:
                pe.wait_ge(plain_lo, BY_DVE.index(piece) + 1)

        def drained(pe, stage):
            if AREAS[stage][1] is None:
                return
            name, arg = AREAS[stage][1]
            if name == "b0":
                pe.wait_ge(b0_ready, arg + 1)
            elif name == "bias":
                pe.wait_ge(bias_ready, arg + 1)
            elif name == "x_in":
                pe.wait_ge(x_full, K * (arg + 1))
            elif name == "w_plain":
                if arg in BY_POOL:
                    pe.wait_ge(plain_copied, BY_POOL.index(arg) + 1)
                else:
                    pe.wait_ge(plain_lo, BY_DVE.index(arg) + 1)
            elif name == "l0":
                pe.wait_ge(x1_full, K * (arg + 1))
            elif name == "l1a":
                pe.wait_ge(h1_full, arg + 1)
            elif name == "l1b":
                pe.wait_ge(s_full, K * (arg + 1))
            elif name == "ln_in":
                wait_norm(pe, arg, BLK - 1)
            elif name == "ln_out":
                pe.wait_ge(x2_full, K * (arg + 1))
            elif name == "lora_b_wi":
                pe.wait_ge(lb_lo, 2 * arg + 1)
            elif name == "lora_b_wo":
                pe.wait_ge(lb_lo, 2 * arg + 2)
            elif name == "w_turn":
                pe.wait_ge(turned, TURNED.index(arg) + 1)
            elif name == "w_lora":
                pe.wait_ge(summed, MERGED.index(arg) + 1)
            else:
                pe.wait_ge(out_copied, K * (layer3_before[phase_of[(3, arg)]] + 1))

        def rows_of(table, i, first, rows):
            return rows[first:first + K, :], table[bass.ds(i, 1)].rearrange("a (r p) -> (a r) p", p=P)

        def b0_load(q, subj, b):
            q.dma_start(b0_raw[:, b, :], b0[bass.ds(subj, 1)].rearrange("a (r p) -> (a r) p", p=P)).then_inc(b0_loaded[b], 16)

        def indexed_bias_loads(q, lang, b):
            done, rows, at = bias_loaded[b], bias_raw[b], 9 * (b == 0)
            for first, table in ((1, b2), (3, gamma), (5, beta)):
                q.dma_start(*rows_of(table, lang, at + first, rows)).then_inc(done, 16)

        def shared_bias_loads(q, done, rows, at):
            if at:
                q.dma_start(rows[0:CHUNKS, :], fc1_b.rearrange("(r p) -> r p", p=P)).then_inc(done, 16)
                q.dma_start(rows[CHUNKS:CHUNKS + 1, :], fc2_b[0:P].rearrange("(r p) -> r p", p=P)).then_inc(done, 16)
            q.dma_start(rows[at + 7:at + 8, 0:SHARED - P],
                        fc2_b[P:SHARED].rearrange("(r p) -> r p", r=1)).then_inc(done, 16)

        def half_row_loads(q, lang, expert, b):
            done, rows, at = rest_loaded[b], bias_raw[b], 9 * (b == 0)
            for half in range(2):
                q.dma_start(rows[at:at + 1, half * A:(half + 1) * A], b1[bass.ds(lang, 1)]).then_inc(done, 16)
            q.dma_start(rows[at + 7:at + 8, SHARED - P:P], ex_b[bass.ds(expert, 1)]).then_inc(done, 16)

        INDEXED_LOADS, REST_LOADS = 3, [6, 4]

        def adapt_loads(q, lang, b):
            q.dma_start(w1_raw[:], w1[bass.ds(lang, 1)].rearrange("a (k p) n -> p (a k) n", p=P)).then_inc(adapt_loaded[b], 16)
            for half in range(2):
                q.dma_start(w2_raw[half * A:(half + 1) * A, :],
                            w2[bass.ds(lang, 1)].rearrange("a p n -> (a p) n")).then_inc(adapt_loaded[b], 16)

        def lora_loads(q, b, own, a_wi, a_wo, b_wi, b_wo):
            for rep in range(3):
                r = rep * RANK2 + own * R
                q.dma_start(la_raw[r:r + R, 0:D], a_wi).then_inc(lora_loaded[b], 16)
                q.dma_start(la_raw[r:r + R, D:D + F], a_wo).then_inc(lora_loaded[b], 16)
            q.dma_start(lb_raw[:, own, 0:CHUNKS, :], b_wi.rearrange("(p j) r -> p j r", j=CHUNKS)).then_inc(lora_loaded[b], 16)
            q.dma_start(lb_raw[:, own, CHUNKS:CHUNKS + K, :], b_wo.rearrange("(p j) r -> p j r", j=K)).then_inc(lora_loaded[b], 16)

        def common_lora_loads(q, b):
            lora_loads(q, b, 0, cwi_a, cwo_a, cwi_b, cwo_b)

        block = ctx.enter_context(nc.Block())

        @block.sync
        def _(sp):
            def load_x(t):
                if t >= 2:
                    sp.wait_ge(pair_full, PAIR_NO[("ln_out", t - 2)] + 1)
                sp.dma_start(x_tok[:, t % 2], x_rows[t * TOKENS:(t + 1) * TOKENS, :].rearrange(
                    "(p k) d -> p k d", k=BLK)).then_inc(x_loaded[t], 16)

            def load_piece(n):
                b, name = PIECES[n]
                slot, done = raw[:, SLOT[PIECES[n]]], raw_loaded[SLOT[PIECES[n]]]
                old = SLOT_BEFORE[PIECES[n]]
                if old:
                    sp.wait_ge(pair_full, PAIR_NO[("w_plain", old)] + 1)
                what, _, half = name.partition("_")
                if name == "w0":
                    sp.dma_start(slot[:, 0:K * D].rearrange("p (c h) -> p c h", c=K),
                                 w0[bass.ds(subj[b], 1)].rearrange("a (c p) h -> p (a c) h", p=P)).then_inc(done, 16)
                elif what in ("fc1", "wi"):
                    source = (fc1_w if what == "fc1" else wi)[int(half) * HALF:(int(half) + 1) * HALF, :]
                    sp.dma_start(slot.rearrange("p (c h) -> p c h", c=CHUNKS // 2),
                                 source.rearrange("(c p) h -> p c h", p=P)).then_inc(done, 16)
                elif name == "fc2_0":
                    sp.dma_start(slot, fc2_w[0:P, :]).then_inc(done, 16)
                elif name == "fc2_1":
                    sp.dma_start(slot[0:SHARED - P], fc2_w[P:SHARED, :]).then_inc(done, 16)
                    sp.dma_start(slot[SHARED - P:P],
                                 ex_w[bass.ds(expert[b], 1)].rearrange("a p h -> (a p) h")).then_inc(done, 16)
                else:
                    sp.dma_start(slot.rearrange("p (c f) -> p c f", c=K),
                                 wo[:, int(half) * HALF:(int(half) + 1) * HALF].rearrange(
                                     "(c p) f -> p c f", p=P)).then_inc(done, 16)

            def load_lora(b):
                if b:
                    sp.wait_ge(la_hi, b)
                    sp.wait_ge(la_lo, b)
                    sp.wait_ge(lb_copied, 2 * b)
                common_lora_loads(sp, b)
                for_wi, for_wo, b_wi, b_wo = (t[bass.ds(subj[b], 1)].rearrange("a r d -> (a r) d")
                                              for t in (ewi_a, ewo_a, ewi_b, ewo_b))
                lora_loads(sp, b, 1, for_wi, for_wo, b_wi, b_wo)

            sp.dma_start(idx[0:1, 0:B], subj_idx.rearrange("(a b) -> a b", a=1)).then_inc(subj_loaded, 16)
            load_x(0)
            for n, source in ((1, lang_idx), (2, exp_idx)):
                sp.dma_start(idx[0:1, n * B:(n + 1) * B], source.rearrange("(a b) -> a b", a=1)).then_inc(idx_loaded, 16)
            subj = [None] * B
            sp.wait_ge(subj_loaded, 16)
            subj[0] = sp.value_load(idx[0:1, 0:1], min_val=0, max_val=w0.shape[0] - 1)
            load_piece(0)
            b0_load(sp, subj[0], 0)
            load_x(1)
            sp.wait_ge(idx_loaded, 32)
            lang = [sp.value_load(idx[0:1, B:B + 1], min_val=0, max_val=w1.shape[0] - 1)]
            indexed_bias_loads(sp, lang[0], 0)
            adapt_loads(sp, lang[0], 0)
            load_piece(1)
            load_piece(2)
            load_piece(3)
            for b in range(1, B):
                subj[b] = sp.value_load(idx[0:1, b:b + 1], min_val=0, max_val=w0.shape[0] - 1)
                lang.append(sp.value_load(idx[0:1, B + b:B + b + 1], min_val=0, max_val=w1.shape[0] - 1))
            expert = [sp.value_load(idx[0:1, 2 * B + b:2 * B + b + 1], min_val=0, max_val=ex_w.shape[0] - 1)
                      for b in range(B)]
            for piece in ("fc2_1", "wi_0", "wi_1"):
                load_piece(PIECE_NO[(0, piece)])
            load_lora(0)
            b0_load(sp, subj[1], 1)
            indexed_bias_loads(sp, lang[1], 1)
            shared_bias_loads(sp, rest_loaded[1], bias_raw[1], 0)
            half_row_loads(sp, lang[1], expert[1], 1)
            for name, arg in PLAN:
                if name in ("w_plain", "w_turn") and PIECE_NO[(0, "wi_1")] < PIECE_NO[arg] + LOADS_AHEAD < len(PIECES) - 1:
                    load_piece(PIECE_NO[arg] + LOADS_AHEAD)
                elif (name, arg) == ("w_lo", (1, "w0")):
                    load_piece(len(PIECES) - 1)
                elif name == "ln_out" and arg + 2 < TILES:
                    load_x(arg + 2)
                elif name == "lora_b_wi" and arg == 0:
                    sp.wait_ge(adapt_hi, 3)
                    sp.wait_ge(adapt_lo, 2)
                    adapt_loads(sp, lang[1], 1)
                    load_lora(1)
                elif name == "out":
                    n = layer3_before[phase_of[(3, arg)]]
                    rows = out_rows[arg * TOKENS:(arg + 1) * TOKENS, :].rearrange("(p i) d -> p i d", i=BLK)
                    for k in range(K):
                        sp.wait_ge(out_copied, K * n + k + 1)
                        sp.dma_start(rows[:, :, k * P:(k + 1) * P], out_tok[:, :, k * P:(k + 1) * P]).then_inc(out_stored, 16)
            sp.wait_ge(out_stored, 16 * K * TILES)

        @block.tensor
        def _(pe):
            mm = nc.tensor.matmul

            def exact(dst, w_hi, w_lo, a_hi, a_lo, start, stop):
                mm(dst, w_hi, a_hi, start=start, stop=False)
                mm(dst, w_hi, a_lo, start=False, stop=False)
                return mm(dst, w_lo, a_hi, start=False, stop=stop)

            def turn(dst, source):
                return nc.tensor.transpose(dst, source, ident[0:source.shape[0], 0:source.shape[0]])

            def keep_busy(bank):
                mm(bank[:, 0:P], ident[:], ident[:], start=True, stop=True)

            pe.wait_ge(ident_ready, 1)
            for n in range(WARM_UP):
                keep_busy(acc[:, 0])

            for stage in PLAN:
                name, arg = stage
                if name in PAIR_STAGES:
                    drained(pe, stage)
                    dst = pair(stage)
                if name == "b0":
                    pe.wait_ge(b0_loaded[arg], 16)
                    turn(dst[:, 0:K], b0_raw[:, arg, :]).then_inc(pair_full, 1)
                elif name == "bias":
                    pe.wait_ge(bias_loaded[arg], 16 * INDEXED_LOADS)
                    pe.wait_ge(rest_loaded[arg], 16 * REST_LOADS[arg])
                    turn(dst[:, 0:bias_raw[arg].shape[0]], bias_raw[arg][:]).then_inc(pair_full, 1)
                elif name == "x_in":
                    pe.wait_ge(x_loaded[arg], 16)
                    for k in range(K):
                        for i in range(BLK):
                            last = turn(dst[:, k * TOKENS + i * P:k * TOKENS + (i + 1) * P],
                                        x_tok[:, arg % 2, i, k * P:(k + 1) * P])
                        if k == 0:
                            last.then_inc(half_full, 1)
                    last.then_inc(pair_full, 1)
                elif name in ("w_plain", "w_turn"):
                    b, piece = arg
                    n = PIECE_NO[arg]
                    slot = raw[:, SLOT[arg]]
                    loads = sum(2 if a[1] == "fc2_1" else 1 for a in PIECES[:n + 1] if SLOT[a] == SLOT[arg])
                    pe.wait_ge(raw_loaded[SLOT[arg]], 16 * loads)
                    view = shaped(dst, piece)
                    if piece[:3] == "fc2":
                        for j in range(CHUNKS):
                            last = turn(view[:, j, :], slot[:, j * P:(j + 1) * P])
                    elif piece[:2] == "wo":
                        for j in range(CHUNKS // 2):
                            for c in range(K):
                                last = turn(view[:, j, c * P:(c + 1) * P], slot[:, c * HALF + j * P:c * HALF + (j + 1) * P])
                    else:
                        for k in range(K):
                            for c in range(K if piece == "w0" else CHUNKS // 2):
                                last = turn(view[:, k, c * P:(c + 1) * P], slot[:, c * D + k * P:c * D + (k + 1) * P])
                    last.then_inc(pair_full, 1)
                elif name in ("lora_b_wi", "lora_b_wo"):
                    pe.wait_ge(lb_copied, 2 * (arg + 1))
                    first, n = (0, CHUNKS) if name == "lora_b_wi" else (CHUNKS, K)
                    for j in range(n):
                        last = turn(dst[0:3 * RANK2, j * P:(j + 1) * P],
                                    lb_rep[:, first + j].rearrange("p a b r -> p (a b r)"))
                    last.then_inc(pair_full, 1)
                elif name == "w_lora":
                    b, piece = arg
                    half = int(piece[3:])
                    pe.wait_ge(la_lo, b + 1)
                    pe.wait_ge(lb_lo, 2 * (b + 1))
                    if piece[:2] == "wi":
                        for k in range(K):
                            last = mm(dst[:, k * HALF:(k + 1) * HALF], la[:, k * P:(k + 1) * P],
                                      lb[:, half * HALF:(half + 1) * HALF], start=True, stop=True)
                    else:
                        for j in range(CHUNKS // 2):
                            f = D + half * HALF + j * P
                            last = mm(dst[:, j * D:(j + 1) * D], la[:, f:f + P], lb[:, F:F + D], start=True, stop=True)
                    last.then_inc(pair_full, 1)
                elif name == "l0":
                    s = arg % RES_SLOTS
                    wait_plain(pe, (arg // PER_BATCH, "w0"))
                    for k in range(K):
                        pe.wait_ge(x_lo, K * arg + k + 1)
                        for c in range(K):
                            last = exact(dst[:, c * TOKENS:(c + 1) * TOKENS], w0_hi[:, k, c * P:(c + 1) * P],
                                         w0_lo[:, k, c * P:(c + 1) * P], res_hi[:, s, k], res_lo[:, s, k],
                                         k == 0, k == K - 1)
                            if k == K - 1 and c == 0:
                                last.then_inc(half_full, 1)
                    last.then_inc(pair_full, 1)
                elif name == "l1a":
                    s = arg % RES_SLOTS
                    pe.wait_ge(adapt_lo, 2 * (arg // PER_BATCH + 1))
                    for k in range(K):
                        pe.wait_ge(x1_lo, K * arg + k + 1)
                        last = exact(dst[:, 0:TOKENS], w1_hi[:, k].rearrange("p a n -> p (a n)"),
                                     w1_lo[:, k].rearrange("p a n -> p (a n)"), res_hi[:, s, k], res_lo[:, s, k],
                                     k == 0, k == K - 1)
                    last.then_inc(pair_full, 1)
                elif name == "l1b":
                    pe.wait_ge(h1_hi_s, arg + 1)
                    for c in range(K):
                        mm(dst[:, c * TOKENS:(c + 1) * TOKENS], w2_both[:, c * P:(c + 1) * P], h1_hi[:],
                           start=True, stop=False)
                    pe.wait_ge(h1_lo_s, arg + 1)
                    for c in range(K):
                        last = mm(dst[:, c * TOKENS:(c + 1) * TOKENS], w2_both[0:A, c * P:(c + 1) * P], h1_lo[:],
                                  start=False, stop=True)
                        if c == 0:
                            last.then_inc(half_full, 1)
                    last.then_inc(pair_full, 1)
                elif name == "ln_in":
                    for k in range(K):
                        pe.wait_ge(s_full, K * arg + k + 1)
                        for i in range(BLK):
                            last = turn(dst[:, i * D + k * P:i * D + (k + 1) * P], xt[:, arg % 2, k, i * P:(i + 1) * P])
                            if (k, i) == (K - 1, BLK // 2 - 1):
                                last.then_inc(half_full, 1)
                    last.then_inc(pair_full, 1)
                elif name == "ln_out":
                    if arg == 0:
                        for n in range(KEEP_WARM):
                            keep_busy(dst)
                    for i in range(BLK):
                        wait_norm(pe, arg, i)
                        for k in range(K):
                            last = turn(dst[:, k * TOKENS + i * P:k * TOKENS + (i + 1) * P],
                                        x_tok[:, arg % 2, i, k * P:(k + 1) * P])
                    last.then_inc(pair_full, 1)
                elif name == "out":
                    for k in range(K):
                        pe.wait_ge(res_full, K * phase_of[(3, arg)] + k + 1)
                        for i in range(BLK):
                            last = turn(dst[:, k * TOKENS + i * P:k * TOKENS + (i + 1) * P],
                                        res[:, arg % RES_SLOTS, k, i * P:(i + 1) * P])
                        if k == 0:
                            last.then_inc(half_full, 1)
                    last.then_inc(pair_full, 1)
                elif name == "up":
                    ph, j = divmod(arg, CHUNKS)
                    layer, t = PHASES[ph]
                    b = t // PER_BATCH
                    s = t % RES_SLOTS
                    if arg == 0:
                        pe.wait_ge(plain_copied, BY_POOL.index((0, "fc2_0")) + 1)
                    if arg >= 2 and arg - 2 in GELUS:
                        pe.wait_ge(hid_full, GELUS.index(arg - 2) + 1)
                    elif arg >= 2:
                        pe.wait_ge(hid_lo_s, arg - 1)
                    if j % (CHUNKS // 2) == 0:
                        half = j // (CHUNKS // 2)
                        if layer == 2:
                            wait_plain(pe, (0, f"fc1_{half}"))
                        else:
                            pe.wait_ge(merged_lo, MERGED.index((b, f"wi_{half}")) + 1)
                    w_hi, w_lo = (fc1_hi, fc1_lo) if layer == 2 else (wi_hi, wi_lo)
                    for k in range(K):
                        if j == 0 and layer == 2:
                            pe.wait_ge(x2_lo, K * t + k + 1)
                        elif j == 0 and k == 0:
                            pe.wait_ge(x3_lo, layer2_before[phase_of[(2, t)]] + 1)
                        last = exact(hid_ps[:, arg % 2], w_hi[:, k, j * P:(j + 1) * P], w_lo[:, k, j * P:(j + 1) * P],
                                     res_hi[:, s, k], res_lo[:, s, k], k == 0, k == K - 1)
                    last.then_inc(up_done, 1)
                elif name == "down":
                    ph, j = divmod(arg, CHUNKS)
                    layer, t = PHASES[ph]
                    b = t // PER_BATCH
                    if layer == 2:
                        if j == 0:
                            wait_plain(pe, (0, "fc2_0"))
                            wait_plain(pe, (b, "fc2_1"))
                        w_hi, w_lo = fc2_hi, fc2_lo
                    else:
                        if j % (CHUNKS // 2) == 0:
                            pe.wait_ge(merged_lo, MERGED.index((b, f"wo_{j // (CHUNKS // 2)}")) + 1)
                        w_hi, w_lo = wo_hi, wo_lo
                    pe.wait_ge(hid_lo_s, arg + 1)
                    for c in range(K):
                        if j == 0 and ph:
                            pe.wait_ge(res_full, K * (ph - 1) + c + 1)
                        last = exact(acc[:, c], w_hi[:, j, c * P:(c + 1) * P], w_lo[:, j, c * P:(c + 1) * P],
                                     hid_hi[:, arg % HID_SLOTS], hid_lo[:, arg % HID_SLOTS], j == 0, j == CHUNKS - 1)
                        if j == CHUNKS - 1 and c < K - 1:
                            last.then_inc(acc_full, 1)
                    last.then_inc(down_done, 1)

        @block.scalar
        def _(act):
            fn = nc.scalar.activation

            act.wait_ge(mhalf_ready, 1)
            fn(table_warm[:], mhalf[:, 0:1], ACT.Gelu)

            for stage in PLAN:
                name, arg = stage
                if name in ("b0", "bias", "lora_b_wi", "lora_b_wo"):
                    source = pair(stage)
                    act.wait_ge(pair_full, PAIR_NO[stage] + 1)
                if name == "b0":
                    fn(bias_of(arg, "b0", 0, K), source[:, 0:K], ACT.Copy).then_inc(b0_ready, 1)
                elif name == "bias":
                    first, n = (0, 17) if arg == 0 else (19, 8)
                    fn(bias[:, first:first + n], source[:, 0:n], ACT.Copy).then_inc(bias_ready, 1)
                elif name == "x_in":
                    s = arg % RES_SLOTS
                    if arg >= RES_SLOTS:
                        act.wait_ge(pair_full, PAIR_NO[("out", arg - RES_SLOTS)] + 1)
                    source = pair(stage)
                    for k in range(K):
                        wait_bank(act, stage, k)
                        fn(res_hi[:, s, k], source[:, k * TOKENS:(k + 1) * TOKENS], ACT.Copy).then_inc(x_hi, 1)
                elif name == "x_copy":
                    source = pair(("x_in", arg))
                    if arg >= 2:
                        act.wait_ge(pair_full, PAIR_NO[("ln_in", arg - 2)] + 1)
                    for k in range(K):
                        act.wait_ge(x_lo, K * arg + k + 1)
                        fn(xt[:, arg % 2, k], source[:, k * TOKENS:(k + 1) * TOKENS], ACT.Copy).then_inc(x_full, 1)
                elif name == "w_hi":
                    b, piece = arg
                    source = pair(("w_plain", arg))
                    act.wait_ge(pair_full, PAIR_NO[("w_plain", arg)] + 1)
                    if piece == "w0" and b:
                        act.wait_ge(pair_full, PAIR_NO[("l0", b * PER_BATCH - 1)] + 1)
                    if piece == "fc2_1" and b:
                        act.wait_ge(down_done, CHUNKS * (phase_of[(2, b * PER_BATCH - 1)] + 1))
                    high = fn(plain_dest(piece)[0], shaped(source, piece), ACT.Copy)
                    if arg in BY_DVE:
                        high.then_inc(plain_hi, 1)
                    else:
                        n = BY_POOL.index(arg)
                        if n >= 2:
                            act.wait_ge(pool_lo, n - 1)
                        fn(merged[:, n % 2], source, ACT.Copy).then_inc(plain_copied, 1)
                elif name == "w_adapt":
                    act.wait_ge(adapt_loaded[arg], 48)
                    if arg:
                        act.wait_ge(pair_full, PAIR_NO[("l1b", arg * PER_BATCH - 1)] + 1)
                    for half in range(2):
                        fn(w1_hi[:, :, half], w1_raw[:], ACT.Copy).then_inc(adapt_hi, 1)
                    fn(w2_both[:], w2_raw[:], ACT.Copy).then_inc(adapt_hi, 1)
                elif name == "x1_hi":
                    s = arg % RES_SLOTS
                    act.wait_ge(pair_full, PAIR_NO[("l0", arg)] + 1)
                    for k in range(K):
                        act.wait_ge(x1_full, K * arg + k + 1)
                        fn(res_hi[:, s, k], res[:, s, k], ACT.Copy).then_inc(x1_hi, 1)
                elif name == "h1":
                    b = arg // PER_BATCH
                    source = pair(("l1a", arg))
                    act.wait_ge(pair_full, PAIR_NO[("l1a", arg)] + 1)
                    act.wait_ge(bias_ready, b + 1)
                    if arg:
                        act.wait_ge(pair_full, PAIR_NO[("l1b", arg - 1)] + 1)
                    fn(h1_hi[:], source[:, 0:TOKENS], ACT.Relu, bias=bias_of(b, "b1")).then_inc(h1_hi_s, 1)
                    fn(h1[:], source[0:A, 0:TOKENS], ACT.Relu, bias=bias_of(b, "b1")[0:A]).then_inc(h1_full, 1)
                elif name == "ln_norm":
                    act.wait_ge(shift_ready, arg + 1)
                    for i in range(BLK // 2, BLK):
                        fn(x_tok[:, arg % 2, i, :], pair(("ln_in", arg))[:, i * D:(i + 1) * D], ACT.Identity,
                           bias=shift[:, i:i + 1], scale=rstd[:, i:i + 1]).then_inc(norm_act, 1)
                elif name == "x2_base":
                    act.wait_ge(s_full, K * (arg + 1))
                    for k in range(K):
                        row = res[:, arg % RES_SLOTS, k]
                        fn(row, row, ACT.Identity, bias=bias_of(arg // PER_BATCH, "beta", k)).then_inc(base_ready, 1)
                elif name == "x2_hi":
                    s = arg % RES_SLOTS
                    for k in range(K):
                        act.wait_ge(x2_full, K * arg + k + 1)
                        fn(res_hi[:, s, k], res[:, s, k], ACT.Copy).then_inc(x2_hi, 1)
                elif name == "lora_a":
                    act.wait_ge(lora_loaded[arg], 16 * LORA_LOADS)
                    if arg:
                        act.wait_ge(pair_full, PAIR_NO[("w_lora", (arg - 1, "wo_1"))] + 1)
                    fn(la[:], la_raw[:], ACT.Copy).then_inc(la_hi, 1)
                elif name in ("lora_b_wi", "lora_b_wo"):
                    first, n, at = (0, CHUNKS, 0) if name == "lora_b_wi" else (CHUNKS, K, F)
                    fn(lb[:, at:at + n * P].rearrange("r (p j) -> r j p", j=n),
                       source[0:3 * RANK2, 0:n * P].rearrange("r (j p) -> r j p", j=n), ACT.Copy,
                       scale=ALPHA).then_inc(lb_hi, 1)
                elif name == "w_split":
                    b, piece = arg
                    n = MERGED.index(arg)
                    act.wait_ge(summed, n + 1)
                    if b:
                        ph = phase_of[(3, b * PER_BATCH - 1)]
                        used = CHUNKS * ph + CHUNKS // 2 * (int(piece[3:]) + 1)
                        act.wait_ge(up_done if piece[:2] == "wi" else down_done, used)
                    fn(merged_dest(piece)[0], shaped(merged[:, n % 2], piece), ACT.Copy).then_inc(merged_hi, 1)
                elif name == "up":
                    ph, j = divmod(arg, CHUNKS)
                    layer, t = PHASES[ph]
                    act.wait_ge(up_done, arg + 1)
                    if arg >= HID_SLOTS:
                        act.wait_ge(down_done, arg - HID_SLOTS + 1)
                    dst = hid_hi[:, arg % HID_SLOTS]
                    if layer == 2:
                        n = GELUS.index(arg)
                        fn(dst, hid_ps[:, arg % 2], ACT.Gelu, bias=bias_fc1(j)).then_inc(hid_hi_s, 1)
                        if n >= 2:
                            act.wait_ge(hid_lo_s, GELUS[n - 2] + 1)
                        fn(hid[:, n % 2], hid_ps[:, arg % 2], ACT.Gelu, bias=bias_fc1(j)).then_inc(hid_full, 1)
                    else:
                        fn(dst, hid_ps[:, arg % 2], ACT.Relu).then_inc(hid_hi_s, 1)
                elif name == "res":
                    layer, t = PHASES[arg]
                    if layer == 2:
                        act.wait_ge(res_full, K * (arg + 1))
                        fn(res_hi[:, t % RES_SLOTS], res[:, t % RES_SLOTS], ACT.Copy).then_inc(x3_hi, 1)
                elif name == "out":
                    n = layer3_before[phase_of[(3, arg)]]
                    if n:
                        act.wait_ge(out_stored, 16 * K * n)
                    for k in range(K):
                        wait_bank(act, stage, k)
                        fn(out_tok[:, :, k * P:(k + 1) * P],
                           pair(stage)[:, k * TOKENS:(k + 1) * TOKENS].rearrange("p (i d) -> p i d", i=BLK),
                           ACT.Copy).then_inc(out_copied, 1)

        @block.vector
        def _(dve):
            v = nc.vector

            def subtract_high(lo, whole, hi):
                return v.tensor_tensor(lo, whole, hi.bitcast(F32), ALU.subtract)

            for stage in PLAN:
                name, arg = stage
                if name in PAIR_STAGES:
                    source = pair(stage)
                if name == "w_lo" and arg in BY_DVE:
                    source = pair(("w_plain", arg))
                    dve.wait_ge(plain_hi, BY_DVE.index(arg) + 1)
                    hi, lo = plain_dest(arg[1])
                    subtract_high(lo, shaped(source, arg[1]), hi).then_inc(plain_lo, 1)
                elif name == "x_in_lo":
                    s = arg % RES_SLOTS
                    source = pair(("x_in", arg))
                    for k in range(K):
                        dve.wait_ge(x_hi, K * arg + k + 1)
                        subtract_high(res_lo[:, s, k], source[:, k * TOKENS:(k + 1) * TOKENS], res_hi[:, s, k]).then_inc(x_lo, 1)
                elif name == "x1":
                    b, s = arg // PER_BATCH, arg % RES_SLOTS
                    source = pair(("l0", arg))
                    dve.wait_ge(b0_ready, b + 1)
                    for k in range(K):
                        wait_bank(dve, ("l0", arg), k)
                        dve.wait_ge(x_full, K * arg + k + 1)
                        v.scalar_tensor_tensor(out=res[:, s, k], in0=source[:, k * TOKENS:(k + 1) * TOKENS],
                                               scalar=bias_of(b, "b0", k), in1=xt[:, arg % 2, k], op0=ALU.add,
                                               op1=ALU.add).then_inc(x1_full, 1)
                elif name == "x1_lo":
                    s = arg % RES_SLOTS
                    for k in range(K):
                        dve.wait_ge(x1_hi, K * arg + k + 1)
                        subtract_high(res_lo[:, s, k], res[:, s, k], res_hi[:, s, k]).then_inc(x1_lo, 1)
                elif name == "h1_lo":
                    dve.wait_ge(h1_full, arg + 1)
                    subtract_high(h1_lo[:], h1[:], h1_hi[0:A]).then_inc(h1_lo_s, 1)
                elif name == "s":
                    b, s = arg // PER_BATCH, arg % RES_SLOTS
                    source = pair(("l1b", arg))
                    dve.wait_ge(bias_ready, b + 1)
                    for k in range(K):
                        wait_bank(dve, ("l1b", arg), k)
                        v.scalar_tensor_tensor(out=xt[:, arg % 2, k], in0=source[:, k * TOKENS:(k + 1) * TOKENS],
                                               scalar=bias_of(b, "b2", k), in1=res[:, s, k], op0=ALU.add,
                                               op1=ALU.add).then_inc(s_full, 1)
                elif name == "ln_in":
                    if arg:
                        dve.wait_ge(rstd_ready, arg)
                    done = (2 * BLK + 1) * arg
                    for i in range(BLK):
                        wait_bank(dve, stage, 2 * i // BLK)
                        v.bn_stats(stats[:, i, :], source[:, i * D:(i + 1) * D]).then_inc(stat_step, 1)
                    dve.wait_ge(stat_step, done + BLK)
                    for i in range(BLK):
                        v.bn_aggr(mv[:, i, :], stats[:, i, :]).then_inc(stat_step, 1)
                    dve.wait_ge(stat_step, done + 2 * BLK)
                    v.tensor_scalar(var_eps[:], mv[:, :, 1], LN_EPS, None, ALU.add).then_inc(stat_step, 1)
                elif name == "ln_norm":
                    dve.wait_ge(rstd_ready, arg + 1)
                    ps = pair(("ln_in", arg))
                    if arg:
                        wait_norm(dve, arg - 1, BLK - 1)
                    v.scalar_tensor_tensor(out=shift[:], in0=mv[:, :, 0], scalar=-1.0, in1=rstd[:], op0=ALU.mult,
                                           op1=ALU.mult).then_inc(shift_ready, 1)
                    for i in range(BLK // 2):
                        v.tensor_scalar(x_tok[:, arg % 2, i, :], ps[:, i * D:(i + 1) * D], mv[:, i, 0:1],
                                        rstd[:, i:i + 1], ALU.subtract, ALU.mult).then_inc(norm_dve, 1)
                elif name == "x2":
                    s = arg % RES_SLOTS
                    source = pair(("ln_out", arg))
                    dve.wait_ge(pair_full, PAIR_NO[("ln_out", arg)] + 1)
                    for k in range(K):
                        dve.wait_ge(base_ready, K * arg + k + 1)
                        v.scalar_tensor_tensor(out=res[:, s, k], in0=source[:, k * TOKENS:(k + 1) * TOKENS],
                                               scalar=bias_of(arg // PER_BATCH, "gamma", k), in1=res[:, s, k],
                                               op0=ALU.mult, op1=ALU.add).then_inc(x2_full, 1)
                elif name == "x2_lo":
                    s = arg % RES_SLOTS
                    for k in range(K):
                        dve.wait_ge(x2_hi, K * arg + k + 1)
                        subtract_high(res_lo[:, s, k], res[:, s, k], res_hi[:, s, k]).then_inc(x2_lo, 1)
                elif name in ("lora_b_wi", "lora_b_wo"):
                    dve.wait_ge(lb_hi, 2 * arg + (name == "lora_b_wo") + 1)
                    first, n, at = (0, CHUNKS, 0) if name == "lora_b_wi" else (CHUNKS, K, F)
                    view = lb[RANK2:2 * RANK2, at:at + n * P].rearrange("r (p j) -> r j p", j=n)
                    v.scalar_tensor_tensor(out=view, in0=source[RANK2:2 * RANK2, 0:n * P].rearrange("r (j p) -> r j p", j=n),
                                           scalar=ALPHA, in1=view.bitcast(F32), op0=ALU.mult,
                                           op1=ALU.subtract).then_inc(lb_lo, 1)
                elif name == "w_turn":
                    dve.wait_ge(pair_full, PAIR_NO[stage] + 1)
                    v.tensor_copy(raw[:, SLOT[arg]], source).then_inc(turned, 1)
                elif name == "w_lora":
                    n = MERGED.index(arg)
                    dve.wait_ge(pair_full, PAIR_NO[stage] + 1)
                    dve.wait_ge(turned, TURNED.index((0, arg[1])) + 1)
                    if n >= 2:
                        dve.wait_ge(merged_lo, n - 1)
                    else:
                        dve.wait_ge(pool_lo, len(BY_POOL))
                    v.tensor_tensor(merged[:, n % 2], source, raw[:, SLOT[(0, arg[1])]], ALU.add).then_inc(summed, 1)
                elif name == "hid_lo":
                    s = arg % HID_SLOTS
                    if arg in GELUS:
                        n = GELUS.index(arg)
                        dve.wait_ge(hid_full, n + 1)
                        subtract_high(hid_lo[:, s], hid[:, n % 2], hid_hi[:, s]).then_inc(hid_lo_s, 1)
                    else:
                        dve.wait_ge(hid_hi_s, arg + 1)
                        v.scalar_tensor_tensor(out=hid_lo[:, s], in0=hid_ps[:, arg % 2], scalar=0.0,
                                               in1=hid_hi[:, s].bitcast(F32), op0=ALU.max,
                                               op1=ALU.subtract).then_inc(hid_lo_s, 1)
                elif name == "res":
                    layer, t = PHASES[arg]
                    s, b = t % RES_SLOTS, t // PER_BATCH
                    for c in range(K):
                        if c < K - 1:
                            dve.wait_ge(acc_full, arg + 1)
                        else:
                            dve.wait_ge(down_done, CHUNKS * (arg + 1))
                        if layer == 2:
                            v.scalar_tensor_tensor(out=res[:, s, c], in0=acc[:, c], scalar=bias_fc2(b, c),
                                                   in1=res[:, s, c], op0=ALU.add, op1=ALU.add).then_inc(res_full, 1)
                        else:
                            v.tensor_tensor(res[:, s, c], acc[:, c], res[:, s, c], ALU.add).then_inc(res_full, 1)
                elif name == "res_lo":
                    layer, t = PHASES[arg]
                    if layer == 2:
                        dve.wait_ge(x3_hi, layer2_before[arg] + 1)
                        s = t % RES_SLOTS
                        subtract_high(res_lo[:, s], res[:, s], res_hi[:, s]).then_inc(x3_lo, 1)

        @block.gpsimd
        def _(pool):
            g = nc.gpsimd
            g.memset(ident[:], 0.0).then_inc(ident_zero, 1)
            g.memset(mhalf[:], -0.5).then_inc(mhalf_ready, 1)
            pool.wait_ge(ident_zero, 1)
            g.affine_select(out=ident[:], in_=ident[:], compare_op=ALU.not_equal, fill=1.0, base=0,
                            pattern=[[-1, P]], channel_multiplier=1).then_inc(ident_ready, 1)
            pool.wait_ge(mhalf_ready, 1)
            shared_bias_loads(pool, rest_loaded[0], bias_raw[0], 9)
            pool.wait_ge(idx_loaded, 32)
            lang, expert = (pool.value_load(idx[0:1, n * B:n * B + 1], min_val=0, max_val=table.shape[0] - 1)
                            for n, table in ((1, w1), (2, ex_w)))
            half_row_loads(pool, lang, expert, 0)

            def subtract_high(lo, whole, hi):
                return g.tensor_tensor(lo, whole, hi.bitcast(F32), ALU.subtract)

            for name, arg in PLAN:
                if name == "ln_in":
                    pool.wait_ge(stat_step, (2 * BLK + 1) * (arg + 1))
                    if arg:
                        wait_norm(pool, arg - 1, BLK - 1)
                    g.tensor_tensor(rstd[:], var_eps[:], mhalf[:], ALU.pow).then_inc(rstd_ready, 1)
                elif name == "lora_a":
                    pool.wait_ge(la_hi, arg + 1)
                    low = slice(2 * RANK2, 3 * RANK2)
                    subtract_high(la[low], la_raw[low], la[low]).then_inc(la_lo, 1)
                    pool.wait_ge(la_lo, arg + 1)
                    if arg:
                        pool.wait_ge(pair_full, PAIR_NO[("lora_b_wo", arg - 1)] + 1)
                    for n in range(2):
                        g.tensor_copy(lb_rep[:, :, :, n, :],
                                      lb_raw[:, n].unsqueeze(2).to_broadcast([P, CHUNKS + K, 3, R])).then_inc(lb_copied, 1)
                elif name == "w_adapt":
                    pool.wait_ge(adapt_hi, 3 * (arg + 1))
                    for half in range(2):
                        last = subtract_high(w1_lo[:, :, half], w1_raw[:], w1_hi[:, :, half])
                    last.then_inc(adapt_lo, 1)
                    pool.wait_ge(adapt_lo, 2 * arg + 1)
                    subtract_high(w2_both[A:2 * A], w2_raw[A:2 * A], w2_both[A:2 * A]).then_inc(adapt_lo, 1)
                    pool.wait_ge(adapt_lo, 2 * (arg + 1))
                elif name == "w_lo" and arg in BY_POOL:
                    n = BY_POOL.index(arg)
                    pool.wait_ge(plain_copied, n + 1)
                    hi, lo = plain_dest(arg[1])
                    subtract_high(lo, shaped(merged[:, n % 2], arg[1]), hi).then_inc(pool_lo, 1)
                elif name == "w_split":
                    n = MERGED.index(arg)
                    pool.wait_ge(merged_hi, n + 1)
                    hi, lo = merged_dest(arg[1])
                    subtract_high(lo, shaped(merged[:, n % 2], arg[1]), hi).then_inc(merged_lo, 1)


_INS = ['x', 'itok_B_0_7', 'itok_B_0_8', 'itok_B_0_15', 'L0_cond_weight', 'L0_cond_bias', 'L1_cond_W1', 'L1_cond_b1',
        'L1_cond_W2', 'L1_cond_b2', 'L1_cond_gamma', 'L1_cond_beta', 'L2_cond_fc1_w', 'L2_cond_fc1_b',
        'L2_cond_fc2_w', 'L2_cond_fc2_b', 'L2_cond_experts_w', 'L2_cond_experts_b', 'L3_cond_wi', 'L3_cond_wo',
        'L3_cond_common_wi_a', 'L3_cond_common_wi_b', 'L3_cond_common_wo_a', 'L3_cond_common_wo_b',
        'L3_cond_experts_wi_a', 'L3_cond_experts_wi_b', 'L3_cond_experts_wo_a', 'L3_cond_experts_wo_b']


def kernel(**inputs):
    import numpy as _np
    import concourse.bacc as _bacc
    from concourse import mybir as _mybir
    from concourse.bass_utils import run_bass_kernel_spmd as _run

    nc = _bacc.Bacc("TRN2", target_bir_lowering=False, num_devices=1)
    arrays, args = {}, []
    for name in _INS:
        a = _np.ascontiguousarray(inputs[name])
        arrays[f"in_{name}_dram"] = a
        args.append(nc.dram_tensor(f"in_{name}_dram", a.shape, _mybir.dt.from_np(a.dtype), kind="ExternalInput").ap())
    args.append(nc.dram_tensor("out_0_dram", inputs["x"].shape, _mybir.dt.float32, kind="ExternalOutput").ap())
    build(nc, *args)
    r = _run(nc, [arrays], core_ids=[0])
    return r.results[0]["out_0_dram"]
```
